# Optimizing a Trainium2 kernel written in Bass

```python
import numpy as np
import jax
import jax.numpy as jnp

def _softmax(x, axis=-1):
    return jax.nn.softmax(x, axis=axis)

def _gelu(x):
    return jax.nn.gelu(x, approximate=True)

def _silu(x):
    return jax.nn.silu(x)

def _sigmoid(x):
    return jax.nn.sigmoid(x)

def _layernorm(x, axis=-1, eps=1e-05):
    m = jnp.mean(x, axis=axis, keepdims=True)
    v = jnp.var(x, axis=axis, keepdims=True)
    return (x - m) / jnp.sqrt(v + eps)

def _scatter_add(tgt, idx, src, axis=0):
    return tgt.at[idx].add(src)

def _segment_sum(src, seg, n):
    return jax.ops.segment_sum(src, seg, n)
kernel_name = 'mk_flamingo_gated_d1_seqx_r4_c52ec3'

def setup_inputs(seed: int=0):
    np.random.seed(seed)
    _w = jnp.asarray

    def _rec_inputs():
        import jax
        import jax.numpy as jnp
        _rk = jax.random.key(seed)
        x = -0.0003929 + 0.9999 * jax.random.normal(jax.random.fold_in(_rk, 1), (32, 128, 256), jnp.float32)
        _lenS = 128 - jax.random.randint(jax.random.fold_in(_rk, 7), (32,), 0, max(1, 128 // 4) + 1, jnp.int32)
        _lenS2 = 128 - jax.random.randint(jax.random.fold_in(_rk, 8), (32,), 0, max(1, 128 // 4) + 1, jnp.int32)
        _ctx_1024P = jax.random.normal(jax.random.fold_in(_rk, 11), (32, 16, 256), jnp.float32)
        _ctx_1024c = jax.random.dirichlet(jax.random.fold_in(_rk, 511), 0.3 * jnp.ones((16,), jnp.float32), (32, 128))
        _ctx_1024t = jnp.einsum('bsk,bkd->bsd', _ctx_1024c, _ctx_1024P)
        _ctx_1024t = _ctx_1024t * jax.lax.rsqrt(jnp.mean(jnp.square(_ctx_1024t)) + 1e-12) * 0.953939
        ctx_1024 = 2.81802e-05 + 1.00001 * (_ctx_1024t + 0.3 * jax.random.normal(jax.random.fold_in(_rk, 611), (32, 128, 256), jnp.float32))
        _g = jax.random.normal(jax.random.fold_in(_rk, 9001), (2, 1), jnp.float32)
        _g = jnp.sign(_g) * jnp.maximum(jnp.abs(_g), 1.0) + (_g == 0) * 1.0
        g_xattn = _g[0]
        g_ffn = _g[1]
        return (x, ctx_1024, g_xattn, g_ffn)
    x, ctx_1024, g_xattn, g_ffn = _rec_inputs()

    def _L0_xattn_setup():
        import jax, jax.numpy as jnp
        import numpy as np
        HEADS = 16

        def _linear(x, w, b):
            return jnp.einsum('bld,od->blo', x, w) + b
        key = jax.random.key(seed)
        ks = jax.random.split(key, 11)
        B, L, QD, KVD = (8, 512, 256, 256)
        s_in = 1.0 / np.sqrt(QD)
        return {'query': jax.random.normal(ks[0], (B, L, QD), jnp.float32), 'key': jax.random.normal(ks[1], (B, L, KVD), jnp.float32), 'value': jax.random.normal(ks[2], (B, L, KVD), jnp.float32), 'wq_w': jax.random.normal(ks[3], (KVD, QD), jnp.float32) * s_in, 'wq_b': jnp.zeros((KVD,), jnp.float32), 'wk_w': jax.random.normal(ks[4], (KVD, KVD), jnp.float32) * s_in, 'wk_b': jnp.zeros((KVD,), jnp.float32), 'wv_w': jax.random.normal(ks[5], (KVD, KVD), jnp.float32) * s_in, 'wv_b': jnp.zeros((KVD,), jnp.float32), 'fo_w': jax.random.normal(ks[6], (QD, KVD), jnp.float32) * s_in, 'fo_b': jnp.zeros((QD,), jnp.float32)}
    _L0_xattn_all = _L0_xattn_setup()
    _L0_xattn_in = {k: v for k, v in _L0_xattn_all.items() if k in ('wq_w', 'wq_b', 'wk_w', 'wk_b', 'wv_w', 'wv_b', 'fo_w', 'fo_b')}
    del _L0_xattn_all

    def _L0_ffn_setup():
        import jax, jax.numpy as jnp
        import numpy as np
        EPS = 1e-05

        @jax.custom_vjp
        def ste_quantize(w):
            scale = jnp.maximum(jnp.mean(jnp.abs(w)), EPS)
            return jnp.clip(jnp.round(w / scale), -1.0, 1.0)

        def _ste_fwd(w):
            return (ste_quantize(w), None)

        def _ste_bwd(_, g):
            return (g,)
        ste_quantize.defvjp(_ste_fwd, _ste_bwd)
        key = jax.random.key(seed)
        k1, k2 = jax.random.split(key)
        x = jax.random.normal(k1, (8, 2048, 256), dtype=jnp.float32)
        weight = jax.random.normal(k2, (256, 256), dtype=jnp.float32) * 0.02
        return {'x': x, 'weight': weight}
    _L0_ffn_all = _L0_ffn_setup()
    _L0_ffn_in = {k: v for k, v in _L0_ffn_all.items() if k in ('weight',)}
    del _L0_ffn_all
    return {'x': x, 'ctx_1024': ctx_1024, 'g_xattn': g_xattn, 'g_ffn': g_ffn, 'L0_xattn_wq_w': _L0_xattn_in['wq_w'], 'L0_xattn_wq_b': _L0_xattn_in['wq_b'], 'L0_xattn_wk_w': _L0_xattn_in['wk_w'], 'L0_xattn_wk_b': _L0_xattn_in['wk_b'], 'L0_xattn_wv_w': _L0_xattn_in['wv_w'], 'L0_xattn_wv_b': _L0_xattn_in['wv_b'], 'L0_xattn_fo_w': _L0_xattn_in['fo_w'], 'L0_xattn_fo_b': _L0_xattn_in['fo_b'], 'L0_ffn_weight': _L0_ffn_in['weight']}

def reference(x, ctx_1024, g_xattn, g_ffn, L0_xattn_wq_w, L0_xattn_wq_b, L0_xattn_wk_w, L0_xattn_wk_b, L0_xattn_wv_w, L0_xattn_wv_b, L0_xattn_fo_w, L0_xattn_fo_b, L0_ffn_weight):
    import jax
    import jax.numpy as jnp

    def _L0_xattn_ref(query, key, value, wq_w, wq_b, wk_w, wk_b, wv_w, wv_b, fo_w, fo_b):
        import jax, jax.numpy as jnp
        import numpy as np
        HEADS = 16

        def _linear(x, w, b):
            return jnp.einsum('bld,od->blo', x, w) + b
        B, Lq, _ = query.shape
        Lk = key.shape[1]
        kvd = wq_w.shape[0]
        head_dim = kvd // HEADS
        q = _linear(query, wq_w, wq_b).reshape(B, Lq, HEADS, head_dim)
        k = _linear(key, wk_w, wk_b).reshape(B, Lk, HEADS, head_dim)
        v = _linear(value, wv_w, wv_b).reshape(B, Lk, HEADS, head_dim)
        scale = 1.0 / jnp.sqrt(jnp.float32(head_dim))
        scores = jnp.einsum('bhid,bhjd->bhij', q, k) * scale
        weights = jax.nn.softmax(scores, axis=-1)
        out = jnp.einsum('bhij,bhjd->bhid', weights, v)
        out = out.reshape(B, Lq, kvd)
        return _linear(out, fo_w, fo_b)

    def _L0_ffn_ref(x, weight):
        import jax, jax.numpy as jnp
        import numpy as np
        EPS = 1e-05

        @jax.custom_vjp
        def ste_quantize(w):
            scale = jnp.maximum(jnp.mean(jnp.abs(w)), EPS)
            return jnp.clip(jnp.round(w / scale), -1.0, 1.0)

        def _ste_fwd(w):
            return (ste_quantize(w), None)

        def _ste_bwd(_, g):
            return (g,)
        ste_quantize.defvjp(_ste_fwd, _ste_bwd)
        w_ternary = ste_quantize(weight)
        scale = jnp.maximum(jnp.mean(jnp.abs(weight)), EPS)
        return jnp.einsum('bsi,oi->bso', x, w_ternary * scale)
    x = x + jnp.tanh(g_xattn[0]) * _L0_xattn_ref(_layernorm(x, axis=-1), ctx_1024, ctx_1024, L0_xattn_wq_w, L0_xattn_wq_b, L0_xattn_wk_w, L0_xattn_wk_b, L0_xattn_wv_w, L0_xattn_wv_b, L0_xattn_fo_w, L0_xattn_fo_b)
    x = x + jnp.tanh(g_ffn[0]) * _L0_ffn_ref(_layernorm(x, axis=-1), L0_ffn_weight)
    return x

_drawn_inputs = setup_inputs


def setup_inputs(seed=0):
    import zlib

    import numpy as np

    out = dict(_drawn_inputs(seed))
    spreads = {'L0_xattn_wq_b': (0.0, 0.35),
     'L0_xattn_wk_b': (0.0, 0.342),
     'L0_xattn_wv_b': (0.0, 0.346),
     'L0_xattn_fo_b': (0.0, 0.1)}
    factors = {}
    for name, (base, spread) in spreads.items():
        noise = np.random.default_rng([zlib.crc32(name.encode()), seed]).standard_normal(out[name].shape)
        drawn = base * np.exp(spread * noise) if base else spread * noise
        out[name] = jnp.asarray(drawn.astype(out[name].dtype))
    for name, factor in factors.items():
        out[name] = (out[name] * factor).astype(out[name].dtype)
    return out
```

```python
from contextlib import ExitStack

import concourse.bass as bass
from concourse import mybir

F32 = mybir.dt.float32
F32R = mybir.dt.float32r
BF16 = mybir.dt.bfloat16
ALU = mybir.AluOpType
ACT = mybir.ActivationFunctionType
AX_X = mybir.AxisListType.X

P = 128
HEADS = 16
GROUP = 4
UNITS = 4
MASKED = -1e30
POOL_CONSTS = 9
LN_EPS = 1e-5
TERNARY_EPS = 1e-5

LAG = dict(ln1=0, transpose=1, project=2, score=7, value=8, out=12, x1t=13, ffn=14)
BODY = 8


class At:

    def __init__(self, c, k=None, per=BODY):
        self.c, self.k, self.per = c, k, per

    def back(self, n):
        return At(self.c - n, self.k, self.per)

    def over(self, n):
        return At(self.c // n, self.k, self.per // n)

    def value(self):
        return self.c if self.k is None else self.k * self.per + self.c


def count(at, per=1, extra=0):
    n = per * (at.c + 1) + extra
    if at.k is None:
        return n
    assert n > 0
    return at.k * (per * at.per) + n


def gated_block(nc, x, ctx, g_xattn, g_ffn, wq, bq, wk, bk, wv, bv, wo, bo, wf, out, qkv_dram, attn_dram):
    B, L, D = x.shape
    HD = D // HEADS
    KC = D // P
    T2 = 2
    SLOTS = L // UNITS // T2
    SQ = T2 * HEADS
    R = L // T2
    SQS = 4
    S4 = SLOTS // SQS
    S8 = SLOTS // 2
    HW = HEADS * L
    assert L == P and D == KC * P and HD == 16 and SQ == 32 and GROUP == UNITS == SQS and B % BODY == 0
    STEPS = B + LAG["ffn"]
    LOOP_FROM = 2 * BODY
    LOOPS = (B - LOOP_FROM) // BODY

    with ExitStack() as es:
        def sb(name, shape, dt=F32):
            return es.enter_context(nc.sbuf_tensor(name, shape, dt))

        def ps(name):
            return es.enter_context(nc.psum_tensor(name, [P, 512], F32))

        def sem(name):
            return es.enter_context(nc.semaphore(name))

        x_in = sb("x_in", [P, 2, D])
        c_in = sb("c_in", [P, 2, D])
        x_res = sb("x_res", [P, 2, D])
        xn = sb("xn", [P, 2, D])
        x1 = sb("x1", [P, 4, D])
        x1n = sb("x1n", [P, 2, D])
        y = sb("y", [P, 2, D])
        xc_t = sb("xc_t", [P, 2, 2, 2 * KC, 2 * L], F32R)
        x1_t = sb("x1_t", [P, 2, 2, KC * L], F32R)
        nat = sb("nat", [P, 2, 3 * KC, 2 * L])
        q_s = sb("q_s", [P, 2, HW])
        k_s = sb("k_s", [P, 2, GROUP, HW])
        v_s = sb("v_s", [P, 2, 2, HEADS, 2 * L // SQS])
        shifted = sb("shifted", [P, SLOTS, SQ])
        probs = sb("probs", [P, SLOTS, SQ])
        probs_t = sb("probs_t", [P, 2, SLOTS, SQ])
        v_t = sb("v_t", [P, S4, GROUP, SQ])
        v_d = sb("v_d", [P, 2, S4 * GROUP, SQS, HD + 1])
        row_max = sb("row_max", [P, SLOTS])
        recip = sb("recip", [P, SLOTS])
        attn = sb("attn", [P, SLOTS * HD])
        attn_t = sb("attn_t", [P, 2, HEADS, R])
        attn_in = sb("attn_in", [P, GROUP, 2, KC, R])
        attn_p = sb("attn_p", [P, 2, KC * L])
        mask_l = sb("mask_l", [32, P], BF16)
        mask_r = sb("mask_r", [32, SLOTS * SQ], BF16)
        stats = sb("stats", [P, 4, 6])
        mv = sb("mv", [P, 4, 2])
        ln_c = sb("ln_c", [P, 4, 3])
        neg_half = sb("neg_half", [P, 1])
        ident = sb("ident", [P, P])
        ones_f = sb("ones_f", [P, P])
        ones_r = sb("ones_r", [P, L], F32R)
        wq_t = sb("wq_t", [P, 2, KC, D], F32R)
        wk_t = sb("wk_t", [P, 2, KC, D], F32R)
        wv_t = sb("wv_t", [P, 2, KC, D], F32R)
        wo_t = sb("wo_t", [P, KC * D])
        wf_t = sb("wf_t", [P, KC * D], F32R)
        bias_raw = sb("bias_raw", [2, D])
        bias_hi = sb("bias_hi", [2, D], F32R)
        bias = sb("bias", [P, D], F32R)
        bias_col = sb("bias_col", [P, 3 * KC])
        row_mask = sb("row_mask", [2, 1])
        gates = sb("gates", [P, 2])
        gates_t = sb("gates_t", [P, 2])
        scal = sb("scal", [P, 8])

        p_tr = ps("p_tr")
        p_x1t = ps("p_x1t")
        p_proj = ps("p_proj")
        p_v = ps("p_v")
        p_score = ps("p_score")
        p_value = ps("p_value")
        p_out = ps("p_out")
        p_ffn = ps("p_ffn")

        w_loaded = sem("w_loaded")
        bias_loaded = sem("bias_loaded")
        gates_loaded = sem("gates_loaded")
        x_loaded = [sem("x_loaded0"), sem("x_loaded1")]
        c_loaded = [sem("c_loaded0"), sem("c_loaded1")]
        res_loaded = [sem("res_loaded0"), sem("res_loaded1")]
        y_stored = [sem("y_stored0"), sem("y_stored1")]
        nat_written = [sem("nat_written0"), sem("nat_written1")]
        stacked = [sem("stacked0"), sem("stacked1")]
        attn_written = [sem(f"attn_written{i}") for i in range(GROUP)]
        attn_loaded = [sem(f"attn_loaded{i}") for i in range(GROUP)]
        zeroed = sem("zeroed")
        const_ready = sem("const_ready")
        dve_const = sem("dve_const")
        w_transposed = sem("w_transposed")
        w_hi = sem("w_hi")
        abs_summed = sem("abs_summed")
        abs_total = sem("abs_total")
        setup_chain = sem("setup_chain")
        w_ready = sem("w_ready")
        gates_tanh = sem("gates_tanh")
        stats1 = sem("stats1")
        mv1 = sem("mv1")
        stats2 = sem("stats2")
        mv2 = sem("mv2")
        ln1_chain = sem("ln1_chain")
        ln2_chain = sem("ln2_chain")
        xn_ready = sem("xn_ready")
        x1n_ready = sem("x1n_ready")
        xc_transposed = sem("xc_transposed")
        xc_hi = sem("xc_hi")
        xc_lo = sem("xc_lo")
        projected = sem("projected")
        v_projected = sem("v_projected")
        nat_ready = sem("nat_ready")
        scored = sem("scored")
        max_done = sem("max_done")
        shift_done = sem("shift_done")
        exp_done = sem("exp_done")
        probs_turned = sem("probs_turned")
        v_turned = sem("v_turned")
        v_placed = sem("v_placed")
        value_done = sem("value_done")
        recip_done = sem("recip_done")
        attn_kept = sem("attn_kept")
        attn_turned = sem("attn_turned")
        attn_ordered = sem("attn_ordered")
        out_done = sem("out_done")
        x1_ready = sem("x1_ready")
        x1_transposed = sem("x1_transposed")
        x1_hi = sem("x1_hi")
        x1_lo = sem("x1_lo")
        ffn_done = sem("ffn_done")
        y_ready = sem("y_ready")

        weights = [wq, wk, wv, wo, wf]
        w_raw = [nat[:, i // 3, i % 3 * 2:i % 3 * 2 + 2, :] for i in range(5)]
        w_bank = [p_proj, p_v, p_score, p_value, p_out]
        q_scale = float(HD) ** -0.5

        def wait_value(eng, s, value, alone):
            if alone:
                eng.compute_val(value)
                eng.wait_ge(const_ready, 1)
            eng.wait_ge(s, value)

        def wait_for(eng, s, at, per=1, extra=0, alone=False):
            if at.k is None:
                if at.c > B - 1:
                    at = At(B - 1)
                if count(at, per, extra) <= 0:
                    return
            wait_value(eng, s, count(at, per, extra), at.k is not None and (alone or eng is nc.gpsimd or eng is nc.sync))

        def wait_parity(eng, sems, at):
            if at.k is None and at.c < 0:
                return
            wait_value(eng, sems[at.c % 2], count(at.over(2), 16), at.k is not None and eng is nc.gpsimd)

        def wait_stacked(eng, a):
            eng.wait_ge(stacked[a.c // GROUP % 2], count(a.over(2 * GROUP), 16 * 5 * GROUP))

        def batch(s, stage):
            t = s.back(LAG[stage])
            return t if t.k is not None or 0 <= t.c < B else None

        def run(eng, step):
            for s in range(LOOP_FROM):
                step(At(s))
            with eng.Fori(0, LOOPS) as k:
                for j in range(BODY):
                    step(At(LOOP_FROM + j, k))
            for s in range(LOOP_FROM + LOOPS * BODY, STEPS + 1):
                step(At(s))

        def rows(dram, t):
            return dram[bass.ds(t.value(), 1), :, :].rearrange("b l d -> l b d")

        block = es.enter_context(nc.Block())

        @block.sync
        def _(sp):
            for i, w in enumerate(weights):
                sp.dma_start(w_raw[i], w.rearrange("(c p) d -> p c d", p=P)).then_inc(w_loaded, 16)
            for r in range(2):
                sp.dma_start(bias_raw[r:r + 1, :], bo.rearrange("(a d) -> a d", a=1)).then_inc(bias_loaded, 16)
            for i, b in enumerate((bq, bk, bv)):
                for c in range(KC):
                    sp.dma_start(bias_col[:, KC * i + c:KC * i + c + 1],
                                 b[c * P:c * P + P].rearrange("(p a) -> p a", a=1)).then_inc(bias_loaded, 16)
            for i, g in enumerate((g_xattn, g_ffn)):
                sp.dma_start(gates[:, i:i + 1],
                             g.rearrange("(a d) -> a d", a=1).to_broadcast([P, 1])).then_inc(gates_loaded, 16)

            def load_x(t):
                wait_for(sp, xn_ready, t.back(2))
                sp.dma_start(x_in[:, t.c % 2:t.c % 2 + 1, :], rows(x, t)).then_inc(x_loaded[t.c % 2], 16)

            def load_c(t):
                wait_for(sp, xc_transposed, t.back(2))
                sp.dma_start(c_in[:, t.c % 2:t.c % 2 + 1, :], rows(ctx, t)).then_inc(c_loaded[t.c % 2], 16)

            def load_res(t):
                wait_for(sp, x1_ready, t.back(2))
                sp.dma_start(x_res[:, t.c % 2:t.c % 2 + 1, :], rows(x, t)).then_inc(res_loaded[t.c % 2], 16)

            def nat_to_stacks(n):
                pair, g = n.over(2), n.over(GROUP)
                wait_for(sp, nat_ready, n, 3)
                b = n.c // 2 % 2
                there = qkv_dram[bass.ds(pair.value(), 1), :, :, :]
                sp.dma_start(there.rearrange("a s p t -> (a p) s t"), nat[:, b, :, :]).then_inc(nat_written[b], 16)
                last = At(n.c // GROUP * GROUP - GROUP - 1, n.k)
                wait_for(sp, scored, last)
                wait_for(sp, v_turned, last, GROUP)
                if n.k is None and n.c < 2 * GROUP:
                    sp.wait_ge(zeroed, 4)
                wait_value(sp, nat_written[b], count(n.over(GROUP), 16), n.k is not None)
                for i in range(2):
                    c, gp = (n.c - 1 + i) % GROUP, g.c % 2
                    rows16 = slice(32 * c, 32 * c + HD)
                    mine = there[:, :, :, i * L:i * L + L]
                    for t2 in range(T2):
                        sp.dma_start(q_s[rows16, gp, t2 * (HW // T2):(t2 + 1) * (HW // T2)
                                         ].rearrange("p (h r) -> p h r", h=HEADS),
                                     mine[:, 0:KC, :, t2 * R:t2 * R + R].rearrange("a s (h p) r -> (a p) (s h) r", p=HD)
                                     ).then_inc(stacked[gp], 16)
                    sp.dma_start(k_s[rows16, gp, c, :].rearrange("p (h t) -> p h t", h=HEADS),
                                 mine[:, KC:2 * KC, :, :].rearrange("a s (h p) t -> (a p) (s h) t", p=HD)
                                 ).then_inc(stacked[gp], 16)
                W = 2 * L // SQS
                for sq in range(SQS):
                    sp.dma_start(v_s[32 * sq:32 * sq + HD, gp, n.c // 2 % 2, :, :],
                                 there[:, 2 * KC:3 * KC, :, sq * W:sq * W + W].rearrange(
                                     "a s (h p) t -> (a p) (s h) t", p=HD)).then_inc(stacked[gp], 16)

            def attn_back(a):
                g = a.over(GROUP)
                wait_for(sp, attn_turned, a)
                for c in range(GROUP + 2):
                    if c < GROUP:
                        b = a.back(GROUP - 1 - c)
                        for par in range(2):
                            lo = 32 * c + HD * par
                            sp.dma_start(attn_dram[bass.ds(b.value(), 1), par, :, :, :].rearrange("a i p r -> (a p) i r"),
                                         attn_t[lo:lo + HD, g.c % 2, :, :]).then_inc(attn_written[c], 16)
                    if c >= 2:
                        b = a.back(GROUP + 1 - c)
                        wait_for(sp, attn_ordered, b.back(GROUP))
                        wait_value(sp, attn_written[c - 2], count(g, 32), g.k is not None)
                        sp.dma_start(attn_in[:, b.c % GROUP, :, :, :].rearrange("p q c r -> p (q c) r"),
                                     attn_dram[bass.ds(b.value(), 1), :, :, :, :].rearrange(
                                         "a q (c i) p r -> (a i p) (q c) r", c=KC)).then_inc(attn_loaded[c - 2], 16)

            def step(s):
                if s.k is not None or s.c < B:
                    load_x(s)
                    load_c(s)
                t = batch(s, "out")
                if t:
                    load_res(t)
                a = s.back(LAG["value"] + 2)
                if (a.k is not None or 0 <= a.c < B) and a.c % GROUP == GROUP - 1:
                    attn_back(a)
                n = s.back(LAG["project"] + 2)
                if (n.k is not None or 0 <= n.c < B) and n.c % 2 == 1:
                    nat_to_stacks(n)
                t = s.back(LAG["ffn"] + 1)
                if t.k is not None or 0 <= t.c < B:
                    wait_for(sp, y_ready, t)
                    sp.dma_start(rows(out, t), y[:, t.c % 2:t.c % 2 + 1, :]).then_inc(y_stored[t.c % 2], 16)

            run(sp, step)
            for i in range(2):
                sp.wait_ge(y_stored[i], 16 * (B // 2))

        @block.gpsimd
        def _(pool):
            pool.memset(ident[:, :], 0.0).then_inc(const_ready, 1)
            pool.memset(neg_half[:, :], -0.5).then_inc(const_ready, 1)
            pool.memset(row_mask[:, :], 0.0).then_inc(const_ready, 1)
            pool.wait_ge(const_ready, 3)
            pool.affine_select(out=ident[:, :], in_=ident[:, :], compare_op=ALU.not_equal, fill=1.0, base=0,
                               pattern=[[-1, P]], channel_multiplier=1).then_inc(const_ready, 1)
            pool.affine_select(out=row_mask[:, :], in_=row_mask[:, :], compare_op=ALU.not_equal, fill=-1.0, base=-1,
                               pattern=[[0, 1]], channel_multiplier=1).then_inc(const_ready, 1)
            pool.memset(mask_l[:, :], 0.0).then_inc(const_ready, 1)
            pool.memset(mask_r[:, :], MASKED).then_inc(const_ready, 1)
            pool.wait_ge(const_ready, 7)
            pool.affine_select(out=mask_l[:, :], in_=mask_l[:, :], compare_op=ALU.not_equal, fill=1.0, base=0,
                               pattern=[[0, GROUP], [-1, T2], [0, HEADS]], channel_multiplier=1).then_inc(const_ready, 1)
            pool.affine_select(out=mask_r[:, :], in_=mask_r[:, :], compare_op=ALU.not_equal, fill=0.0, base=0,
                               pattern=[[0, SLOTS], [-1, T2], [0, HEADS]], channel_multiplier=1).then_inc(const_ready, 1)
            pool.wait_ge(const_ready, 9)
            pool.memset(q_s[:, :, :], 0.0).then_inc(zeroed, 1)
            pool.memset(v_s[:, :, :, :, :], 1.0).then_inc(zeroed, 1)
            pool.memset(v_d[:, :, :, :, :], 0.0).then_inc(zeroed, 1)

            def layer_norm(chain, src, dst, slot, t, base, per):
                c = ln_c[:, slot, :]
                nc.gpsimd.tensor_scalar(c[:, 0:1], mv[:, slot, 1:2], LN_EPS, None, ALU.add).then_inc(chain, 1)
                wait_for(pool, chain, t, per, base + 1 - per)
                nc.gpsimd.tensor_tensor(c[:, 1:2], c[:, 0:1], neg_half[:, :], ALU.pow).then_inc(chain, 1)
                wait_for(pool, chain, t, per, base + 2 - per)
                nc.gpsimd.tensor_scalar(c[:, 2:3], mv[:, slot, 0:1], c[:, 1:2], -1.0, ALU.mult, ALU.mult
                                        ).then_inc(chain, 1)
                wait_for(pool, chain, t, per, base + 3 - per)
                return nc.gpsimd.tensor_scalar(dst, src, c[:, 1:2], c[:, 2:3], ALU.mult, ALU.add)

            def step(s):
                t = batch(s, "ln1")
                if t:
                    wait_for(pool, mv1, t)
                    wait_parity(pool, x_loaded, t)
                    wait_for(pool, xc_transposed, t.back(2))
                    layer_norm(ln1_chain, x_in[:, t.c % 2, :], xn[:, t.c % 2, :], t.c % 2, t, 0, 3
                               ).then_inc(xn_ready, 1)
                t = batch(s, "out")
                if t:
                    wait_for(pool, mv2, t)
                    wait_for(pool, x1_ready, t)
                    wait_for(pool, x1_transposed, t.back(2))
                    layer_norm(ln2_chain, x1[:, t.c % 4, :], x1n[:, t.c % 2, :], 2 + t.c % 2, t, 0, 3
                               ).then_inc(x1n_ready, 1)

            run(pool, step)

        @block.scalar
        def _(act):
            act.wait_ge(gates_loaded, 32)
            act.activation(gates_t[:, :], gates[:, :], ACT.Tanh).then_inc(gates_tanh, 1)
            act.wait_ge(w_loaded, 16 * 5)
            act.activation(shifted[:, :, :].rearrange("p s q -> p (s q)"), w_raw[4].rearrange("p c d -> p (c d)"), ACT.Abs,
                           accum_out=scal[:, 0:1]).then_inc(abs_summed, 1)
            for i, (w, scale) in enumerate(((wq_t, q_scale), (wk_t, 1.0), (wv_t, 1.0))):
                act.wait_ge(w_transposed, i + 1)
                act.activation(w[:, 0, :, :].rearrange("p c d -> p (c d)"), w_bank[i][:, :], ACT.Copy,
                               scale=scale).then_inc(w_hi, 1)
            act.wait_ge(w_transposed, 4)
            act.activation(wo_t[:, :], w_bank[3][:, :], ACT.Copy).then_inc(w_hi, 1)

            def step(s):
                t = batch(s, "transpose")
                if t:
                    wait_for(act, xc_transposed, t)
                    old = At(t.c // 2 * 2 - 3, t.k)
                    wait_for(act, projected, old)
                    wait_for(act, v_projected, old)
                    o = t.c % 2 * L
                    act.activation(xc_t[:, t.c // 2 % 2, 0, :, o:o + L],
                                   p_tr[:, :].rearrange("p (b l) -> p b l", b=2 * KC), ACT.Copy).then_inc(xc_hi, 1)
                a = batch(s, "score")
                if a:
                    wait_for(act, shift_done, a)
                    wait_for(act, probs_turned, a.back(1))
                    act.activation(probs[:, :, :], shifted[:, :, :], ACT.Exp).then_inc(exp_done, 1)
                n = batch(s, "project")
                if n:
                    b, which = n.c // 2 % 2, n.c % 2
                    wait_for(act, projected, n)
                    if n.k is not None or n.c >= GROUP:
                        act.wait_ge(nat_written[b], count(At(n.c // GROUP - 1, n.k, n.per // GROUP), 16))
                    if n.k is None and n.c == 0:
                        act.wait_ge(w_transposed, 5)
                        act.wait_ge(dve_const, 4)
                        act.wait_ge(bias_loaded, 16 * (2 + 3 * KC))
                    for c in range(KC):
                        i = KC * which + c
                        act.activation(nat[:, b, i, :], p_proj[:, 2 * L * c:2 * L * (c + 1)], ACT.Identity,
                                       bias=bias_col[:, i:i + 1]).then_inc(nat_ready, 1)
                    i = 2 * KC + which
                    wait_for(act, v_projected, n)
                    act.activation(nat[:, b, i, :].rearrange("p (q m s) -> p m q s", q=SQS, s=S4),
                                   p_v[:, 0:2 * L].rearrange("p (m q s) -> p m q s", q=SQS, s=S4), ACT.Identity,
                                   bias=bias_col[:, i:i + 1]).then_inc(nat_ready, 1)
                if a:
                    wait_for(act, v_turned, a, GROUP)
                    wait_for(act, value_done, a.back(2))
                    if s.k is None and a.c < 2:
                        act.wait_ge(zeroed, 4)
                    for sq in range(SQS):
                        h = slice(32 * sq, 32 * sq + 32)
                        act.activation(v_d[h, a.c % 2, :, sq, :],
                                       v_t[h, :, :, 0:HD + 1].rearrange("p s c d -> p (s c) d"), ACT.Copy
                                       ).then_inc(v_placed, 1)
                t = batch(s, "x1t")
                if t:
                    wait_for(act, x1_transposed, t)
                    wait_for(act, ffn_done, t.back(2))
                    act.activation(x1_t[:, t.c % 2, 0, :], p_x1t[:, 0:KC * L], ACT.Copy).then_inc(x1_hi, 1)
                t = batch(s, "out")
                if t:
                    act.wait_ge(attn_loaded[t.c % GROUP], count(t.over(GROUP), 16))
                    wait_for(act, out_done, t.back(2))
                    act.activation(attn_p[:, t.c % 2, :].rearrange("p (m q s) -> p q m s", q=2, s=S4),
                                   attn_in[:, t.c % GROUP, :, :, :].rearrange("p q c (m s) -> p q (c m) s", s=S4), ACT.Copy).then_inc(attn_ordered, 1)

            run(act, step)

        @block.vector
        def _(dve):
            dve.memset(ones_f[:, :], 1.0).then_inc(dve_const, 1)
            dve.memset(bias[:, :].bitcast(F32), 0.0).then_inc(dve_const, 1)
            dve.memset(k_s[:, :, :, :], 0.0).then_inc(zeroed, 1)
            dve.wait_ge(dve_const, 2)
            dve.tensor_copy(ones_r[:, 0:L], ones_f[:, :]).then_inc(dve_const, 1)
            dve.wait_ge(bias_loaded, 16 * (2 + 3 * KC))
            dve.wait_ge(const_ready, 5)
            dve.tensor_scalar(bias_col[:, 0:KC], bias_col[:, 0:KC], q_scale, None, ALU.mult).then_inc(dve_const, 1)
            dve.tensor_copy(bias_hi[:, :], bias_raw[:, :]).then_inc(dve_const, 1)
            dve.wait_ge(dve_const, 5)
            dve.scalar_tensor_tensor(out=bias[0:2, :], in0=bias_hi[:, :].bitcast(F32), scalar=row_mask[:, 0:1],
                                     in1=bias_raw[:, :], op0=ALU.mult, op1=ALU.add).then_inc(dve_const, 1)
            for i, (w, scale) in enumerate(((wq_t, q_scale), (wk_t, 1.0), (wv_t, 1.0))):
                dve.wait_ge(w_hi, i + 1)
                dve.scalar_tensor_tensor(out=w[:, 1, :, :].rearrange("p c d -> p (c d)"), in0=w_bank[i][:, :],
                                         scalar=scale, in1=w[:, 0, :, :].rearrange("p c d -> p (c d)").bitcast(F32),
                                         op0=ALU.mult, op1=ALU.subtract).then_inc(w_ready, 1)
            dve.wait_ge(abs_total, 1)
            dve.tensor_scalar(scal[:, 1:2], p_ffn[:, 0:1], 1.0 / (D * D), TERNARY_EPS, ALU.mult, ALU.max
                              ).then_inc(setup_chain, 1)
            dve.wait_ge(setup_chain, 1)
            dve.tensor_scalar(scal[:, 2:3], scal[:, 1:2], 0.5, None, ALU.mult).then_inc(setup_chain, 1)
            dve.tensor_scalar(scal[:, 3:4], scal[:, 1:2], -0.5, None, ALU.mult).then_inc(setup_chain, 1)
            dve.wait_ge(gates_tanh, 1)
            dve.tensor_tensor(scal[:, 4:5], scal[:, 1:2], gates_t[:, 1:2], ALU.mult).then_inc(setup_chain, 1)
            dve.wait_ge(setup_chain, 4)
            dve.wait_ge(w_transposed, 5)
            above, below = (p[:, :, :].rearrange("p s q -> p (s q)") for p in (shifted, probs))
            dve.tensor_scalar(above, w_bank[4][:, :], scal[:, 2:3], None, ALU.is_gt).then_inc(setup_chain, 1)
            dve.tensor_scalar(below, w_bank[4][:, :], scal[:, 3:4], None, ALU.is_lt).then_inc(setup_chain, 1)
            dve.wait_ge(setup_chain, 6)
            dve.tensor_tensor(wf_t[:, :], above, below, ALU.subtract).then_inc(w_ready, 1)

            def step(s):
                tx = batch(s, "ln1")
                if tx:
                    wait_parity(dve, x_loaded, tx)
                    wait_for(dve, xn_ready, tx.back(2))
                    dve.bn_stats(stats[:, tx.c % 2, :], x_in[:, tx.c % 2, :]).then_inc(stats1, 1)
                a = batch(s, "score")
                if a:
                    if a.c % UNITS == 0:
                        wait_stacked(dve, a)
                    wait_for(dve, v_placed, a.back(1), SQS)
                    o = S4 * (a.c % UNITS)
                    for c in range(GROUP):
                        v = v_s[:, a.c // UNITS % 2, c // 2, :, c % 2 * R // 2:(c % 2 + 1) * R // 2]
                        dve.transpose(v_t[:, :, c, :],
                                      v.rearrange("p h (t r) -> p r t h", t=T2)[:, o:o + S4, :, :]
                                      ).then_inc(v_turned, 1)
                if tx:
                    wait_for(dve, stats1, tx, alone=True)
                    dve.bn_aggr(mv[:, tx.c % 2, :], stats[:, tx.c % 2, :]).then_inc(mv1, 1)
                av = batch(s, "value")
                if av:
                    out3 = p_value[:, 0:SLOTS * (HD + 1)].rearrange("p (s d) -> p s d", s=SLOTS)
                    wait_for(dve, value_done, av)
                    dve.reciprocal(recip[:, :].rearrange("p (s a) -> p s a", a=1), out3[:, :, HD:HD + 1]
                                   ).then_inc(recip_done, 1)
                t = batch(s, "transpose")
                if t:
                    o = t.c % 2 * L
                    wait_for(dve, xc_hi, t)
                    dve.tensor_tensor(xc_t[:, t.c // 2 % 2, 1, :, o:o + L],
                                      p_tr[:, :].rearrange("p (b l) -> p b l", b=2 * KC),
                                      xc_t[:, t.c // 2 % 2, 0, :, o:o + L].bitcast(F32), ALU.subtract
                                      ).then_inc(xc_lo, 1)
                if av:
                    wait_for(dve, recip_done, av)
                    dve.tensor_tensor(attn[:, :].rearrange("p (s d) -> p s d", s=SLOTS), out3[:, :, 0:HD],
                                      recip[:, :].rearrange("p (s a) -> p s a", a=1).to_broadcast([P, SLOTS, HD]),
                                      ALU.mult).then_inc(attn_kept, 1)
                if a:
                    wait_for(dve, scored, a)
                    dve.tensor_reduce(row_max[:, :], p_score[:, :].rearrange("p (s q) -> p s q", s=SLOTS), AX_X,
                                      ALU.max).then_inc(max_done, 1)
                if av:
                    wait_for(dve, attn_kept, av)
                    if av.c % UNITS == 0 and (av.k is not None or av.c >= 2 * GROUP):
                        for c in range(GROUP):
                            dve.wait_ge(attn_written[c], count(av.over(GROUP).back(2), 32))
                    to = attn_t[:, av.c // UNITS % 2, :, :].rearrange("p i (t r) -> p r t i", t=T2)
                    u = av.c % UNITS
                    dve.transpose(to[:, S8 * u:S8 * u + S8, :, :], attn[:, :]).then_inc(attn_turned, 1)
                if a:
                    wait_for(dve, max_done, a)
                    wait_for(dve, exp_done, a.back(1))
                    dve.tensor_tensor(shifted[:, :, :], p_score[:, :].rearrange("p (s q) -> p s q", s=SLOTS),
                                      row_max[:, :].rearrange("p (s a) -> p s a", a=1).to_broadcast([P, SLOTS, SQ]),
                                      ALU.subtract).then_inc(shift_done, 1)
                t = batch(s, "ffn")
                if t:
                    wait_for(dve, ffn_done, t)
                    wait_parity(dve, y_stored, t.back(2))
                    wait_for(dve, x1_ready, t)
                    dve.scalar_tensor_tensor(out=y[:, t.c % 2, :], in0=p_ffn[:, 0:D], scalar=scal[:, 4:5],
                                             in1=x1[:, t.c % 4, :], op0=ALU.mult, op1=ALU.add).then_inc(y_ready, 1)
                if a:
                    wait_for(dve, exp_done, a)
                    wait_for(dve, value_done, a.back(2))
                    dve.transpose(probs_t[:, a.c % 2, :, :].rearrange("p s q -> p (s q)"),
                                  probs[:, :, :].rearrange("p s q -> p (s q)")).then_inc(probs_turned, 1)
                t = batch(s, "x1t")
                if t:
                    wait_for(dve, x1_hi, t)
                    dve.tensor_tensor(x1_t[:, t.c % 2, 1, :], p_x1t[:, 0:KC * L],
                                      x1_t[:, t.c % 2, 0, :].bitcast(F32), ALU.subtract).then_inc(x1_lo, 1)
                t = batch(s, "out")
                if t:
                    wait_for(dve, out_done, t)
                    wait_parity(dve, res_loaded, t)
                    wait_for(dve, y_ready, t.back(4))
                    dve.scalar_tensor_tensor(out=x1[:, t.c % 4, :], in0=p_out[:, 0:D], scalar=gates_t[:, 0:1],
                                             in1=x_res[:, t.c % 2, :], op0=ALU.mult, op1=ALU.add
                                             ).then_inc(x1_ready, 1)
                    wait_for(dve, x1_ready, t)
                    wait_for(dve, x1n_ready, t.back(2))
                    dve.bn_stats(stats[:, 2 + t.c % 2, :], x1[:, t.c % 4, :]).then_inc(stats2, 1)
                    wait_for(dve, stats2, t, alone=True)
                    dve.bn_aggr(mv[:, 2 + t.c % 2, :], stats[:, 2 + t.c % 2, :]).then_inc(mv2, 1)

            run(dve, step)

        @block.tensor
        def _(pe):
            pe.wait_ge(const_ready, 4)
            pe.wait_ge(w_loaded, 16 * 5)
            for i in range(5):
                for kc in range(KC):
                    for oc in range(KC):
                        o = kc * D + oc * P
                        last = pe.transpose(w_bank[i][:, o:o + P], w_raw[i][:, oc, kc * P:kc * P + P], ident[:, :])
                last.then_inc(w_transposed, 1)
            pe.wait_ge(abs_summed, 1)
            pe.wait_ge(dve_const, 1)
            pe.matmul(p_ffn[:, 0:1], ones_f[:, :], scal[:, 0:1], start=True, stop=True).then_inc(abs_total, 1)
            pe.wait_ge(const_ready, POOL_CONSTS)
            pe.wait_ge(dve_const, 6)
            pe.wait_ge(w_hi, 4)
            pe.wait_ge(w_ready, 4)

            def values(a):
                b = a.c % 2
                wait_for(pe, v_placed, a, SQS)
                wait_for(pe, attn_kept, a.back(1))
                wait_for(pe, probs_turned, a)
                cells = p_value[:, 0:SLOTS * (HD + 1)].rearrange("p (q s d) -> p s q d", q=2, s=S4)
                for s4 in range(S4):
                    for c in range(GROUP):
                        last = pe.matmul(cells[32 * c:32 * c + SQ, s4, :, :], probs_t[:, b, GROUP * s4 + c, :],
                                         v_d[:, b, GROUP * s4 + c, :, :].rearrange("p q d -> p (q d)"),
                                         start=True, stop=True)
                last.then_inc(value_done, 1)

            def scores(a):
                gp, u = a.c // UNITS % 2, a.c % UNITS
                if u == 0:
                    wait_stacked(pe, a)
                wait_for(pe, shift_done, a.back(1))
                pe.matmul(p_score[:, :], mask_l[:, :], mask_r[:, :], start=True, stop=False)
                for s4 in range(S4):
                    for sq in range(SQS):
                        r = SLOTS * u + S4 * sq + s4
                        q = q_s[:, gp, :].rearrange("p (a r) -> p a r", r=R)[:, :, r]
                        k = k_s[:, gp, :, :].rearrange("p c (h t r) -> p c t h r", h=HEADS, t=T2)[:, :, :, :, r]
                        last = pe.matmul(p_score[32 * sq:32 * sq + SQ, L * s4:L * (s4 + 1)], q, k, start=False,
                                         stop=(s4 == S4 - 1))
                last.then_inc(scored, 1)

            PARTS = ((0, 0), (0, 1), (1, 0))

            def step(s):
                a = batch(s, "value")
                if a:
                    values(a)
                t = batch(s, "transpose")
                if t:
                    wait_for(pe, xn_ready, t)
                    wait_parity(pe, c_loaded, t)
                    wait_for(pe, xc_lo, t.back(1))
                    for i in range(2 * KC):
                        src = (xn, c_in)[i // KC][:, t.c % 2, i % KC * P:i % KC * P + P]
                        last = pe.transpose(p_tr[:, i * L:(i + 1) * L], src, ident[:, :])
                    last.then_inc(xc_transposed, 1)
                a = batch(s, "score")
                if a:
                    scores(a)
                t = batch(s, "ffn")
                if t:
                    wait_for(pe, x1_lo, t)
                    wait_for(pe, y_ready, t.back(1))
                    for kc in range(KC):
                        for part in range(2):
                            last = pe.matmul(p_ffn[:, 0:D], x1_t[:, t.c % 2, part, kc * L:(kc + 1) * L],
                                             wf_t[:, kc * D:(kc + 1) * D], start=(kc + part == 0),
                                             stop=(kc == KC - 1 and part == 1))
                    last.then_inc(ffn_done, 1)
                n = batch(s, "project")
                if n:
                    w, src = ((wq_t, 0), (wk_t, KC))[n.c % 2]
                    pair = n.c // 2 % 2
                    wait_for(pe, xc_lo, At(n.c // 2 * 2 + 1, n.k))
                    wait_for(pe, nat_ready, n.back(1), 3)
                    for oc in range(KC + 1):
                        if oc == KC:
                            w, src, to, o = wv_t, KC, p_v[:, 0:2 * L], n.c % 2 * P
                        else:
                            to, o = p_proj[:, oc * 2 * L:(oc + 1) * 2 * L], oc * P
                        for kc in range(KC):
                            for ws, ms in PARTS:
                                last = pe.matmul(to, w[:, ws, kc, o:o + P], xc_t[:, pair, ms, src + kc, :],
                                                 start=(kc == 0 and (ws, ms) == PARTS[0]),
                                                 stop=(kc == KC - 1 and (ws, ms) == PARTS[-1]))
                        if oc >= KC - 1:
                            last.then_inc(v_projected if oc == KC else projected, 1)
                t = batch(s, "x1t")
                if t:
                    wait_for(pe, x1n_ready, t)
                    wait_for(pe, x1_lo, t.back(1))
                    for kc in range(KC):
                        last = pe.transpose(p_x1t[:, kc * L:(kc + 1) * L], x1n[:, t.c % 2, kc * P:kc * P + P],
                                            ident[:, :])
                    last.then_inc(x1_transposed, 1)
                t = batch(s, "out")
                if t:
                    wait_for(pe, x1_ready, t.back(1))
                    pe.matmul(p_out[:, 0:D], ones_r[:, 0:L], bias[:, :], start=True, stop=False)
                    wait_for(pe, attn_ordered, t)
                    for kc in range(KC):
                        last = pe.matmul(p_out[:, 0:D], attn_p[:, t.c % 2, kc * L:(kc + 1) * L],
                                         wo_t[:, kc * D:(kc + 1) * D], start=False, stop=(kc == KC - 1))
                    last.then_inc(out_done, 1)

            run(pe, step)


_INS = ["x", "ctx_1024", "g_xattn", "g_ffn", "L0_xattn_wq_w", "L0_xattn_wq_b", "L0_xattn_wk_w", "L0_xattn_wk_b",
        "L0_xattn_wv_w", "L0_xattn_wv_b", "L0_xattn_fo_w", "L0_xattn_fo_b", "L0_ffn_weight"]


def kernel(**inputs):
    import concourse.bacc as _bacc
    import numpy as _np
    from concourse.bass_utils import run_bass_kernel_spmd as _run

    nc = _bacc.Bacc("TRN2", target_bir_lowering=False, num_devices=1)
    arrays, args = {}, []
    for name in _INS:
        a = _np.ascontiguousarray(inputs[name])
        arrays[f"in_{name}"] = a
        args.append(nc.dram_tensor(f"in_{name}", a.shape, mybir.dt.from_np(a.dtype), kind="ExternalInput").ap())
    args.append(nc.dram_tensor("out_x", inputs["x"].shape, F32, kind="ExternalOutput").ap())
    batches, tokens, dim = inputs["x"].shape
    for name, shape in (("qkv", (batches // 2, 3 * dim // P, P, 2 * tokens)),
                        ("attn", (batches, 2, HEADS, dim // HEADS, tokens // 2))):
        args.append(nc.dram_tensor(f"scratch_{name}", shape, F32, kind="Internal").ap())
    gated_block(nc, *args)
    r = _run(nc, [arrays], core_ids=[0])
    return r.results[0]["out_x"]
```

```python
from contextlib import ExitStack

import concourse.bass as bass
from concourse import mybir

F32 = mybir.dt.float32
F32R = mybir.dt.float32r
BF16 = mybir.dt.bfloat16
ALU = mybir.AluOpType
ACT = mybir.ActivationFunctionType
AX_X = mybir.AxisListType.X

P = 128
HEADS = 16
GROUP = 4
UNITS = 4
MASKED = -1e30
POOL_CONSTS = 9
LN_EPS = 1e-5
TERNARY_EPS = 1e-5

LAG = dict(ln1=0, transpose=1, project=2, score=7, value=8, out=12, x1t=13, ffn=14)
BODY = 8


class At:

    def __init__(self, c, k=None, per=BODY):
        self.c, self.k, self.per = c, k, per

    def back(self, n):
        return At(self.c - n, self.k, self.per)

    def over(self, n):
        return At(self.c // n, self.k, self.per // n)

    def value(self):
        return self.c if self.k is None else self.k * self.per + self.c


def count(at, per=1, extra=0):
    n = per * (at.c + 1) + extra
    if at.k is None:
        return n
    assert n > 0
    return at.k * (per * at.per) + n


def gated_block(nc, x, ctx, g_xattn, g_ffn, wq, bq, wk, bk, wv, bv, wo, bo, wf, out, q_dram, k_dram, v_dram,
                attn_dram):
    B, L, D = x.shape
    HD = D // HEADS
    KC = D // P
    T2 = 2
    SLOTS = L // UNITS // T2
    SQ = T2 * HEADS
    R = L // T2
    SQS = 4
    S4 = SLOTS // SQS
    S8 = SLOTS // 2
    HW = HEADS * L
    assert L == P and D == KC * P and HD == 16 and SQ == 32 and GROUP == UNITS == SQS and B % BODY == 0
    STEPS = B + LAG["ffn"]
    LOOP_FROM = 2 * BODY
    LOOPS = (B - LOOP_FROM) // BODY

    with ExitStack() as es:
        def sb(name, shape, dt=F32):
            return es.enter_context(nc.sbuf_tensor(name, shape, dt))

        def ps(name):
            return es.enter_context(nc.psum_tensor(name, [P, 512], F32))

        def sem(name):
            return es.enter_context(nc.semaphore(name))

        x_in = sb("x_in", [P, 2, D])
        c_in = sb("c_in", [P, 2, D])
        x_res = sb("x_res", [P, 2, D])
        xn = sb("xn", [P, 2, D])
        x1 = sb("x1", [P, 4, D])
        x1n = sb("x1n", [P, 2, D])
        y = sb("y", [P, 2, D])
        xc_t = sb("xc_t", [P, 2, 2, 2 * KC, 2 * L], F32R)
        x1_t = sb("x1_t", [P, 2, 2, KC * L], F32R)
        W2 = KC * 2 * L
        nat = sb("nat", [P, 2, 3 * W2])
        q_s = sb("q_s", [P, 2, HW])
        k_s = sb("k_s", [P, 2, GROUP, HW])
        v_s = sb("v_s", [P, 2, 2, HEADS, 2 * L // SQS])
        shifted = sb("shifted", [P, SLOTS, SQ])
        probs = sb("probs", [P, SLOTS, SQ])
        probs_t = sb("probs_t", [P, 2, SLOTS, SQ])
        v_t = sb("v_t", [P, S4, GROUP, SQ])
        v_d = sb("v_d", [P, 2, S4 * GROUP, SQS, HD + 1])
        row_max = sb("row_max", [P, SLOTS])
        recip = sb("recip", [P, SLOTS])
        attn = sb("attn", [P, SLOTS * HD])
        attn_t = sb("attn_t", [P, 2, HEADS, R])
        attn_in = sb("attn_in", [P, GROUP, 2, KC, R])
        attn_p = sb("attn_p", [P, 2, KC * L])
        mask_l = sb("mask_l", [32, P], BF16)
        mask_r = sb("mask_r", [32, SLOTS * SQ], BF16)
        stats = sb("stats", [P, 4, 6])
        mv = sb("mv", [P, 4, 2])
        ln_c = sb("ln_c", [P, 4, 3])
        neg_half = sb("neg_half", [P, 1])
        ident = sb("ident", [P, P])
        ones_f = sb("ones_f", [P, P])
        ones_r = sb("ones_r", [P, L], F32R)
        wq_t = sb("wq_t", [P, 2, KC, D], F32R)
        wk_t = sb("wk_t", [P, 2, KC, D], F32R)
        wv_t = sb("wv_t", [P, 2, KC, D], F32R)
        wo_t = sb("wo_t", [P, KC * D])
        wf_t = sb("wf_t", [P, KC * D], F32R)
        bias_raw = sb("bias_raw", [2, D])
        bias_hi = sb("bias_hi", [2, D], F32R)
        bias = sb("bias", [P, D], F32R)
        bias_col = sb("bias_col", [P, 3 * KC])
        row_mask = sb("row_mask", [2, 1])
        gates = sb("gates", [P, 2])
        gates_t = sb("gates_t", [P, 2])
        scal = sb("scal", [P, 8])

        p_tr = ps("p_tr")
        p_x1t = ps("p_x1t")
        p_proj = ps("p_proj")
        p_v = ps("p_v")
        p_score = ps("p_score")
        p_value = ps("p_value")
        p_out = ps("p_out")
        p_ffn = ps("p_ffn")

        w_loaded = sem("w_loaded")
        bias_loaded = sem("bias_loaded")
        gates_loaded = sem("gates_loaded")
        x_loaded = [sem("x_loaded0"), sem("x_loaded1")]
        c_loaded = [sem("c_loaded0"), sem("c_loaded1")]
        res_loaded = [sem("res_loaded0"), sem("res_loaded1")]
        y_stored = [sem("y_stored0"), sem("y_stored1")]
        q_written = [sem("q_written0"), sem("q_written1")]
        k_written = [sem("k_written0"), sem("k_written1")]
        v_written = [sem("v_written0"), sem("v_written1")]
        stacked = [sem("stacked0"), sem("stacked1")]
        v_stacked = [sem("v_stacked0"), sem("v_stacked1")]
        attn_written = sem("attn_written")
        attn_loaded = [sem(f"attn_loaded{i}") for i in range(GROUP)]
        zeroed = sem("zeroed")
        k_zeroed = sem("k_zeroed")
        const_ready = sem("const_ready")
        dve_const = sem("dve_const")
        wo_ordered = sem("wo_ordered")
        w_transposed = sem("w_transposed")
        w_hi = sem("w_hi")
        abs_summed = sem("abs_summed")
        abs_total = sem("abs_total")
        setup_chain = sem("setup_chain")
        w_ready = sem("w_ready")
        gates_tanh = sem("gates_tanh")
        stats1 = sem("stats1")
        mv1 = sem("mv1")
        stats2 = sem("stats2")
        mv2 = sem("mv2")
        ln1_chain = sem("ln1_chain")
        ln2_chain = sem("ln2_chain")
        xn_ready = sem("xn_ready")
        x1n_ready = sem("x1n_ready")
        xc_transposed = sem("xc_transposed")
        xc_hi = sem("xc_hi")
        xc_lo = sem("xc_lo")
        projected = sem("projected")
        v_projected = sem("v_projected")
        nat_ready = sem("nat_ready")
        scored = sem("scored")
        max_done = sem("max_done")
        shift_done = sem("shift_done")
        exp_done = sem("exp_done")
        probs_turned = sem("probs_turned")
        v_turned = sem("v_turned")
        v_placed = sem("v_placed")
        value_done = sem("value_done")
        recip_done = sem("recip_done")
        attn_kept = sem("attn_kept")
        attn_turned = sem("attn_turned")
        attn_ordered = sem("attn_ordered")
        out_done = sem("out_done")
        x1_ready = sem("x1_ready")
        x1_transposed = sem("x1_transposed")
        x1_hi = sem("x1_hi")
        x1_lo = sem("x1_lo")
        ffn_done = sem("ffn_done")
        y_ready = sem("y_ready")

        weights = [wq, wk, wv, wo, wf]
        w_raw = [nat[:, i // 3, i % 3 * W2:(i % 3 + 1) * W2].rearrange("p (c d) -> p c d", c=KC) for i in range(5)]
        wo_raw = attn_t[:, 0, 0:KC * D // R, :].rearrange("p i r -> p (i r)").rearrange("p (c d) -> p c d", c=KC)
        w_bank = [p_proj, p_v, p_score, p_value, p_out]
        q_scale = float(HD) ** -0.5

        def wait_value(eng, s, value, alone):
            if alone:
                eng.compute_val(value)
                eng.wait_ge(const_ready, 1)
            eng.wait_ge(s, value)

        def wait_for(eng, s, at, per=1, extra=0, alone=False):
            if at.k is None:
                if at.c > B - 1:
                    at = At(B - 1)
                if count(at, per, extra) <= 0:
                    return
            wait_value(eng, s, count(at, per, extra), at.k is not None and (alone or eng is nc.gpsimd or eng is nc.sync))

        def wait_parity(eng, sems, at):
            if at.k is None and at.c < 0:
                return
            wait_value(eng, sems[at.c % 2], count(at.over(2), 16), at.k is not None and eng is nc.gpsimd)

        def wait_stacked(eng, sems, a):
            per = 16 * (GROUP if sems is v_stacked else 2 * GROUP)
            eng.wait_ge(sems[a.c // GROUP % 2], count(a.over(2 * GROUP), per))

        def batch(s, stage):
            t = s.back(LAG[stage])
            return t if t.k is not None or 0 <= t.c < B else None

        def run(eng, step):
            for s in range(LOOP_FROM):
                step(At(s))
            with eng.Fori(0, LOOPS) as k:
                for j in range(BODY):
                    step(At(LOOP_FROM + j, k))
            for s in range(LOOP_FROM + LOOPS * BODY, STEPS + 1):
                step(At(s))

        def rows(dram, t):
            return dram[bass.ds(t.value(), 1), :, :].rearrange("b l d -> l b d")

        block = es.enter_context(nc.Block())

        @block.sync
        def _(sp):
            def load_x(t):
                wait_for(sp, xn_ready, t.back(2))
                sp.dma_start(x_in[:, t.c % 2:t.c % 2 + 1, :], rows(x, t)).then_inc(x_loaded[t.c % 2], 16)

            def load_c(t):
                wait_for(sp, xc_transposed, t.back(2))
                sp.dma_start(c_in[:, t.c % 2:t.c % 2 + 1, :], rows(ctx, t)).then_inc(c_loaded[t.c % 2], 16)

            for t in range(2):
                load_x(At(t))
                load_c(At(t))
            for i, w in enumerate(weights):
                sp.dma_start(w_raw[i], w.rearrange("(c p) d -> p c d", p=P)).then_inc(w_loaded, 16)
            for r in range(2):
                sp.dma_start(bias_raw[r:r + 1, :], bo.rearrange("(a d) -> a d", a=1)).then_inc(bias_loaded, 16)
            for i, b in enumerate((bq, bk, bv)):
                for c in range(KC):
                    sp.dma_start(bias_col[:, KC * i + c:KC * i + c + 1],
                                 b[c * P:c * P + P].rearrange("(p a) -> p a", a=1)).then_inc(bias_loaded, 16)
            for i, g in enumerate((g_xattn, g_ffn)):
                sp.dma_start(gates[:, i:i + 1],
                             g.rearrange("(a d) -> a d", a=1).to_broadcast([P, 1])).then_inc(gates_loaded, 16)

            def load_res(t):
                wait_for(sp, x1_ready, t.back(2))
                sp.dma_start(x_res[:, t.c % 2:t.c % 2 + 1, :], rows(x, t)).then_inc(res_loaded[t.c % 2], 16)

            def write_nat(n):
                b, p = n.c // 2 % 2, bass.ds(n.over(2).value(), 1)
                wait_for(sp, nat_ready, n, 3)
                if n.c % 2 == 0:
                    sp.dma_start(q_dram[p, :, :, :].rearrange("a m p r -> (a p) m r"),
                                 nat[:, b, 0:W2].rearrange("p (m r) -> p m r", r=R)).then_inc(q_written[b], 16)
                    return
                for dram, o, written in ((k_dram, W2, k_written), (v_dram, 2 * W2, v_written)):
                    sp.dma_start(dram[p, :, :, :].rearrange("a c p t -> (a p) c t"),
                                 nat[:, b, o:o + W2].rearrange("p (c t) -> p c t", c=KC)).then_inc(written[b], 16)

            def read_stacks(n):
                pair, g = n.over(2), n.over(GROUP)
                b, gp, at = n.c // 2 % 2, g.c % 2, bass.ds(pair.value(), 1)
                last = At(n.c // GROUP * GROUP - GROUP - 1, n.k)
                wait_for(sp, scored, last)
                if n.k is None and n.c < 2 * GROUP:
                    sp.wait_ge(zeroed, 3)
                    sp.wait_ge(k_zeroed, n.c + 1)
                batches = range(n.c // 2 * 2 % GROUP, n.c // 2 * 2 % GROUP + 2)
                wait_value(sp, q_written[b], count(g, 16), n.k is not None)
                for i, c in enumerate(batches):
                    sp.dma_start(q_s[32 * c:32 * c + HD, gp, :].rearrange("p (m r) -> p m r", r=R),
                                 q_dram[at, i * T2 * KC:(i + 1) * T2 * KC, :, :].rearrange(
                                     "a m (h p) r -> (a p) (m h) r", p=HD)).then_inc(stacked[gp], 16)
                wait_value(sp, k_written[b], count(g, 16), n.k is not None)
                for i, c in enumerate(batches):
                    sp.dma_start(k_s[32 * c:32 * c + HD, gp, c, :].rearrange("p (h t) -> p h t", h=HEADS),
                                 k_dram[at, :, :, i * L:i * L + L].rearrange("a s (h p) t -> (a p) (s h) t", p=HD)
                                 ).then_inc(stacked[gp], 16)
                if n.c % GROUP == GROUP - 1:
                    wait_for(sp, v_turned, last, GROUP)
                    wait_value(sp, v_written[0], count(g, 16), n.k is not None)
                    wait_value(sp, v_written[1], count(g, 16), n.k is not None)
                    pairs = v_dram[bass.ds(n.back(GROUP - 1).over(2).value(), 2), :, :, :]
                    W = 2 * L // SQS
                    for sq in range(SQS):
                        sp.dma_start(v_s[32 * sq:32 * sq + HD, gp, :, :, :].rearrange("p a h t -> p (a h) t"),
                                     pairs[:, :, :, sq * W:sq * W + W].rearrange("a s (h p) t -> p (a s h) t", p=HD)
                                     ).then_inc(v_stacked[gp], 16)

            def attn_back(a):
                g = a.over(GROUP)
                wait_for(sp, attn_turned, a)
                sp.dma_start(attn_dram[bass.ds(g.value(), 1), :, :].rearrange("a p m -> (a p) m"),
                             attn_t[:, g.c % 2, :, :].rearrange("p i r -> p (i r)")).then_inc(attn_written, 16)
                wait_value(sp, attn_written, count(g, 16), g.k is not None)
                there = attn_dram[bass.ds(g.value(), 1), :, :].rearrange("a p m -> (a p m)").rearrange(
                    "(b m p r) -> b p m r", b=GROUP, m=2 * KC, r=R)
                for c in range(GROUP):
                    wait_for(sp, attn_ordered, a.back(2 * GROUP - 1 - c))
                    sp.dma_start(attn_in[:, c, :, :, :].rearrange("p q c r -> p (q c) r"), there[c, :, :, :]
                                 ).then_inc(attn_loaded[c], 16)

            def step(s):
                n = s.back(LAG["project"] + 2)
                n = n if n.k is not None or 0 <= n.c < B else None
                if n:
                    write_nat(n)
                if s.k is not None or 2 <= s.c < B:
                    load_x(s)
                    load_c(s)
                t = batch(s, "out")
                if t:
                    load_res(t)
                if n and n.c % 2 == 1:
                    read_stacks(n)
                t = s.back(LAG["ffn"] + 1)
                if t.k is not None or 0 <= t.c < B:
                    wait_for(sp, y_ready, t)
                    sp.dma_start(rows(out, t), y[:, t.c % 2:t.c % 2 + 1, :]).then_inc(y_stored[t.c % 2], 16)
                a = s.back(LAG["value"] + 1)
                if (a.k is not None or 0 <= a.c < B) and a.c % GROUP == GROUP - 1:
                    attn_back(a)

            run(sp, step)
            for i in range(2):
                sp.wait_ge(y_stored[i], 16 * (B // 2))

        @block.gpsimd
        def _(pool):
            pool.memset(ident[:, :], 0.0).then_inc(const_ready, 1)
            pool.memset(neg_half[:, :], -0.5).then_inc(const_ready, 1)
            pool.memset(row_mask[:, :], 0.0).then_inc(const_ready, 1)
            pool.wait_ge(const_ready, 3)
            pool.affine_select(out=ident[:, :], in_=ident[:, :], compare_op=ALU.not_equal, fill=1.0, base=0,
                               pattern=[[-1, P]], channel_multiplier=1).then_inc(const_ready, 1)
            pool.affine_select(out=row_mask[:, :], in_=row_mask[:, :], compare_op=ALU.not_equal, fill=-1.0, base=-1,
                               pattern=[[0, 1]], channel_multiplier=1).then_inc(const_ready, 1)
            pool.memset(mask_l[:, :], 0.0).then_inc(const_ready, 1)
            pool.memset(mask_r[:, :], MASKED).then_inc(const_ready, 1)
            pool.wait_ge(const_ready, 7)
            pool.affine_select(out=mask_l[:, :], in_=mask_l[:, :], compare_op=ALU.not_equal, fill=1.0, base=0,
                               pattern=[[0, GROUP], [-1, T2], [0, HEADS]], channel_multiplier=1).then_inc(const_ready, 1)
            pool.affine_select(out=mask_r[:, :], in_=mask_r[:, :], compare_op=ALU.not_equal, fill=0.0, base=0,
                               pattern=[[0, SLOTS], [-1, T2], [0, HEADS]], channel_multiplier=1).then_inc(const_ready, 1)
            pool.wait_ge(const_ready, 9)

            def layer_norm(chain, src, dst, slot, t, base, per):
                c = ln_c[:, slot, :]
                nc.gpsimd.tensor_scalar(c[:, 0:1], mv[:, slot, 1:2], LN_EPS, None, ALU.add).then_inc(chain, 1)
                wait_for(pool, chain, t, per, base + 1 - per)
                nc.gpsimd.tensor_tensor(c[:, 1:2], c[:, 0:1], neg_half[:, :], ALU.pow).then_inc(chain, 1)
                wait_for(pool, chain, t, per, base + 2 - per)
                nc.gpsimd.tensor_scalar(c[:, 2:3], mv[:, slot, 0:1], c[:, 1:2], -1.0, ALU.mult, ALU.mult
                                        ).then_inc(chain, 1)
                wait_for(pool, chain, t, per, base + 3 - per)
                return nc.gpsimd.tensor_scalar(dst, src, c[:, 1:2], c[:, 2:3], ALU.mult, ALU.add)

            def step(s):
                t = batch(s, "ln1")
                if t:
                    wait_for(pool, mv1, t)
                    wait_parity(pool, x_loaded, t)
                    wait_for(pool, xc_transposed, t.back(2))
                    layer_norm(ln1_chain, x_in[:, t.c % 2, :], xn[:, t.c % 2, :], t.c % 2, t, 0, 3
                               ).then_inc(xn_ready, 1)
                t = batch(s, "out")
                if t:
                    wait_for(pool, mv2, t)
                    wait_for(pool, x1_ready, t)
                    wait_for(pool, x1_transposed, t.back(2))
                    layer_norm(ln2_chain, x1[:, t.c % 4, :], x1n[:, t.c % 2, :], 2 + t.c % 2, t, 0, 3
                               ).then_inc(x1n_ready, 1)
                if s.k is None and s.c < 3:
                    stack, fill = ((q_s[:, :, :], 0.0), (v_s[:, :, :, :, :], 1.0), (v_d[:, :, :, :, :], 0.0))[s.c]
                    pool.memset(stack, fill).then_inc(zeroed, 1)

            run(pool, step)

        @block.scalar
        def _(act):
            for i, (w, scale) in enumerate(((wq_t, q_scale), (wk_t, 1.0), (wv_t, 1.0))):
                act.wait_ge(w_transposed, i + 1)
                act.activation(w[:, 0, :, :].rearrange("p c d -> p (c d)"), w_bank[i][:, :], ACT.Copy,
                               scale=scale).then_inc(w_hi, 1)
            act.wait_ge(w_transposed, 4)
            act.activation(wo_t[:, :], w_bank[3][:, :], ACT.Copy).then_inc(w_hi, 1)
            act.wait_ge(gates_loaded, 32)
            act.activation(gates_t[:, :], gates[:, :], ACT.Tanh).then_inc(gates_tanh, 1)
            act.wait_ge(w_loaded, 16 * 5)
            act.activation(shifted[:, :, :].rearrange("p s q -> p (s q)"), w_raw[4].rearrange("p c d -> p (c d)"), ACT.Abs,
                           accum_out=scal[:, 0:1]).then_inc(abs_summed, 1)

            def order_attention(t):
                act.wait_ge(attn_loaded[t.c % GROUP], count(t.over(GROUP), 16))
                wait_for(act, out_done, t.back(2))
                act.activation(attn_p[:, t.c % 2, :].rearrange("p (m q s) -> p q m s", q=2, s=S4),
                               attn_in[:, t.c % GROUP, :, :, :].rearrange("p q c (m s) -> p q (c m) s", s=S4), ACT.Copy).then_inc(attn_ordered, 1)

            def step(s):
                t = batch(s, "transpose")
                if t:
                    wait_for(act, xc_transposed, t)
                    old = At(t.c // 2 * 2 - 3, t.k)
                    wait_for(act, projected, old)
                    wait_for(act, v_projected, old)
                    o = t.c % 2 * L
                    act.activation(xc_t[:, t.c // 2 % 2, 0, :, o:o + L],
                                   p_tr[:, :].rearrange("p (b l) -> p b l", b=2 * KC), ACT.Copy).then_inc(xc_hi, 1)
                a = batch(s, "value")
                if a:
                    wait_for(act, v_turned, a, GROUP)
                    wait_for(act, value_done, a.back(2))
                    if s.k is None and a.c < 2:
                        act.wait_ge(zeroed, 3)
                    for sq in range(SQS):
                        h = slice(32 * sq, 32 * sq + 32)
                        act.activation(v_d[h, a.c % 2, :, sq, :],
                                       v_t[h, :, :, 0:HD + 1].rearrange("p s c d -> p (s c) d"), ACT.Copy
                                       ).then_inc(v_placed, 1)
                a = batch(s, "score")
                if a:
                    wait_for(act, shift_done, a)
                    wait_for(act, probs_turned, a.back(1))
                    act.activation(probs[:, :, :], shifted[:, :, :], ACT.Exp).then_inc(exp_done, 1)
                t = batch(s, "out")
                if t and t.c % GROUP > 0:
                    order_attention(t)
                t = batch(s, "x1t")
                if t:
                    wait_for(act, x1_transposed, t)
                    wait_for(act, ffn_done, t.back(2))
                    act.activation(x1_t[:, t.c % 2, 0, :], p_x1t[:, 0:KC * L], ACT.Copy).then_inc(x1_hi, 1)
                t = batch(s, "out")
                if t and t.c % GROUP == 0:
                    order_attention(t)
                n = batch(s, "project")
                if n:
                    b, which = n.c // 2 % 2, n.c % 2
                    wait_for(act, projected, n)
                    if n.k is not None or n.c >= GROUP:
                        for written in ((q_written,), (k_written, v_written))[which]:
                            act.wait_ge(written[b], count(n.over(GROUP).back(1), 16))
                    if n.k is None and n.c == 0:
                        act.wait_ge(w_transposed, 5)
                        act.wait_ge(dve_const, 4)
                        act.wait_ge(bias_loaded, 16 * (2 + 3 * KC))
                    for c in range(KC):
                        i = KC * which + c
                        to = nat[:, b, which * W2:(which + 1) * W2]
                        if which == 0:
                            to = to.rearrange("p (m c r) -> p c m r", c=KC, r=R)[:, c, :, :]
                        else:
                            to = to.rearrange("p (c m r) -> p c m r", c=KC, r=R)[:, c, :, :]
                        act.activation(to, p_proj[:, 2 * L * c:2 * L * (c + 1)].rearrange("p (m r) -> p m r", r=R),
                                       ACT.Identity, bias=bias_col[:, i:i + 1]).then_inc(nat_ready, 1)
                    i = 2 * KC + which
                    wait_for(act, v_projected, n)
                    act.activation(nat[:, b, i * 2 * L:(i + 1) * 2 * L].rearrange("p (q m s) -> p m q s", q=SQS, s=S4),
                                   p_v[:, 0:2 * L].rearrange("p (m q s) -> p m q s", q=SQS, s=S4), ACT.Identity,
                                   bias=bias_col[:, i:i + 1]).then_inc(nat_ready, 1)

            run(act, step)

        @block.vector
        def _(dve):
            dve.memset(ones_f[:, :], 1.0).then_inc(dve_const, 1)
            dve.memset(bias[:, :].bitcast(F32), 0.0).then_inc(dve_const, 1)
            dve.wait_ge(w_loaded, 16 * 5)
            dve.tensor_copy(wo_raw.rearrange("p c (d i) -> p c d i", i=HEADS),
                            w_raw[3].rearrange("p c (i d) -> p c d i", i=HEADS)).then_inc(wo_ordered, 1)
            dve.wait_ge(dve_const, 2)
            dve.tensor_copy(ones_r[:, 0:L], ones_f[:, :]).then_inc(dve_const, 1)
            dve.wait_ge(bias_loaded, 16 * (2 + 3 * KC))
            dve.wait_ge(const_ready, 5)
            dve.tensor_scalar(bias_col[:, 0:KC], bias_col[:, 0:KC], q_scale, None, ALU.mult).then_inc(dve_const, 1)
            dve.tensor_copy(bias_hi[:, :], bias_raw[:, :]).then_inc(dve_const, 1)
            dve.wait_ge(dve_const, 5)
            dve.scalar_tensor_tensor(out=bias[0:2, :], in0=bias_hi[:, :].bitcast(F32), scalar=row_mask[:, 0:1],
                                     in1=bias_raw[:, :], op0=ALU.mult, op1=ALU.add).then_inc(dve_const, 1)
            for i, (w, scale) in enumerate(((wq_t, q_scale), (wk_t, 1.0), (wv_t, 1.0))):
                dve.wait_ge(w_hi, i + 1)
                dve.scalar_tensor_tensor(out=w[:, 1, :, :].rearrange("p c d -> p (c d)"), in0=w_bank[i][:, :],
                                         scalar=scale, in1=w[:, 0, :, :].rearrange("p c d -> p (c d)").bitcast(F32),
                                         op0=ALU.mult, op1=ALU.subtract).then_inc(w_ready, 1)

            def ternary_weights():
                dve.wait_ge(abs_total, 1)
                dve.tensor_scalar(scal[:, 1:2], p_ffn[:, 0:1], 1.0 / (D * D), TERNARY_EPS, ALU.mult, ALU.max
                                  ).then_inc(setup_chain, 1)
                dve.wait_ge(setup_chain, 1)
                dve.tensor_scalar(scal[:, 2:3], scal[:, 1:2], 0.5, None, ALU.mult).then_inc(setup_chain, 1)
                dve.tensor_scalar(scal[:, 3:4], scal[:, 1:2], -0.5, None, ALU.mult).then_inc(setup_chain, 1)
                dve.wait_ge(gates_tanh, 1)
                dve.tensor_tensor(scal[:, 4:5], scal[:, 1:2], gates_t[:, 1:2], ALU.mult).then_inc(setup_chain, 1)
                dve.wait_ge(setup_chain, 4)
                dve.wait_ge(w_transposed, 5)
                above, below = (p[:, :, :].rearrange("p s q -> p (s q)") for p in (shifted, probs))
                dve.tensor_scalar(above, w_bank[4][:, :], scal[:, 2:3], None, ALU.is_gt).then_inc(setup_chain, 1)
                dve.tensor_scalar(below, w_bank[4][:, :], scal[:, 3:4], None, ALU.is_lt).then_inc(setup_chain, 1)
                dve.wait_ge(setup_chain, 6)
                dve.tensor_tensor(wf_t[:, :], above, below, ALU.subtract).then_inc(w_ready, 1)

            def stats_of_x(t):
                wait_parity(dve, x_loaded, t)
                wait_for(dve, xn_ready, t.back(2))
                dve.bn_stats(stats[:, t.c % 2, :], x_in[:, t.c % 2, :]).then_inc(stats1, 1)

            def turn_values(a):
                if a.c % UNITS == 0:
                    wait_stacked(dve, v_stacked, a)
                wait_for(dve, v_placed, a.back(1), SQS)
                o = S4 * (a.c % UNITS)
                for c in range(GROUP):
                    v = v_s[:, a.c // UNITS % 2, c // 2, :, c % 2 * R // 2:(c % 2 + 1) * R // 2]
                    dve.transpose(v_t[:, :, c, :],
                                  v.rearrange("p h (t r) -> p r t h", t=T2)[:, o:o + S4, :, :]).then_inc(v_turned, 1)

            def step(s):
                tx, a = batch(s, "ln1"), batch(s, "score")
                early = s.k is None and s.c < LAG["score"]
                if tx and early:
                    stats_of_x(tx)
                t = batch(s, "transpose")
                if t:
                    o = t.c % 2 * L
                    wait_for(dve, xc_hi, t)
                    dve.tensor_tensor(xc_t[:, t.c // 2 % 2, 1, :, o:o + L],
                                      p_tr[:, :].rearrange("p (b l) -> p b l", b=2 * KC),
                                      xc_t[:, t.c // 2 % 2, 0, :, o:o + L].bitcast(F32), ALU.subtract
                                      ).then_inc(xc_lo, 1)
                if tx and not early:
                    stats_of_x(tx)
                if a:
                    wait_for(dve, scored, a)
                    dve.tensor_reduce(row_max[:, :], p_score[:, :].rearrange("p (s q) -> p s q", s=SLOTS), AX_X,
                                      ALU.max).then_inc(max_done, 1)
                if tx:
                    wait_for(dve, stats1, tx, alone=True)
                    dve.bn_aggr(mv[:, tx.c % 2, :], stats[:, tx.c % 2, :]).then_inc(mv1, 1)
                if a:
                    wait_for(dve, max_done, a)
                    wait_for(dve, exp_done, a.back(1))
                    dve.tensor_tensor(shifted[:, :, :], p_score[:, :].rearrange("p (s q) -> p s q", s=SLOTS),
                                      row_max[:, :].rearrange("p (s a) -> p s a", a=1).to_broadcast([P, SLOTS, SQ]),
                                      ALU.subtract).then_inc(shift_done, 1)
                av = batch(s, "value")
                if av:
                    out3 = p_value[:, 0:SLOTS * (HD + 1)].rearrange("p (s d) -> p s d", s=SLOTS)
                    wait_for(dve, value_done, av)
                    dve.reciprocal(recip[:, :].rearrange("p (s a) -> p s a", a=1), out3[:, :, HD:HD + 1]
                                   ).then_inc(recip_done, 1)
                t = batch(s, "ffn")
                if t:
                    wait_for(dve, ffn_done, t)
                    wait_parity(dve, y_stored, t.back(2))
                    wait_for(dve, x1_ready, t)
                    dve.scalar_tensor_tensor(out=y[:, t.c % 2, :], in0=p_ffn[:, 0:D], scalar=scal[:, 4:5],
                                             in1=x1[:, t.c % 4, :], op0=ALU.mult, op1=ALU.add).then_inc(y_ready, 1)
                if av:
                    wait_for(dve, recip_done, av)
                    dve.tensor_tensor(attn[:, :].rearrange("p (s d) -> p s d", s=SLOTS), out3[:, :, 0:HD],
                                      recip[:, :].rearrange("p (s a) -> p s a", a=1).to_broadcast([P, SLOTS, HD]),
                                      ALU.mult).then_inc(attn_kept, 1)
                if a:
                    wait_for(dve, exp_done, a)
                    wait_for(dve, value_done, a.back(2))
                    dve.transpose(probs_t[:, a.c % 2, :, :].rearrange("p s q -> p (s q)"),
                                  probs[:, :, :].rearrange("p s q -> p (s q)")).then_inc(probs_turned, 1)
                if av:
                    wait_for(dve, attn_kept, av)
                    if av.c % UNITS == 0 and (av.k is not None or av.c >= 2 * GROUP):
                        dve.wait_ge(attn_written, count(av.over(GROUP).back(2), 16))
                    to = attn_t[:, av.c // UNITS % 2, :, :].rearrange("p i (t r) -> p r t i", t=T2)
                    u = av.c % UNITS
                    dve.transpose(to[:, S8 * u:S8 * u + S8, :, :], attn[:, :]).then_inc(attn_turned, 1)
                t = batch(s, "x1t")
                if t:
                    wait_for(dve, x1_hi, t)
                    dve.tensor_tensor(x1_t[:, t.c % 2, 1, :], p_x1t[:, 0:KC * L],
                                      x1_t[:, t.c % 2, 0, :].bitcast(F32), ALU.subtract).then_inc(x1_lo, 1)
                if a:
                    turn_values(a)
                t = batch(s, "out")
                if t:
                    wait_for(dve, out_done, t)
                    wait_parity(dve, res_loaded, t)
                    wait_for(dve, y_ready, t.back(4))
                    dve.scalar_tensor_tensor(out=x1[:, t.c % 4, :], in0=p_out[:, 0:D], scalar=gates_t[:, 0:1],
                                             in1=x_res[:, t.c % 2, :], op0=ALU.mult, op1=ALU.add
                                             ).then_inc(x1_ready, 1)
                    wait_for(dve, x1_ready, t)
                    wait_for(dve, x1n_ready, t.back(2))
                    dve.bn_stats(stats[:, 2 + t.c % 2, :], x1[:, t.c % 4, :]).then_inc(stats2, 1)
                    wait_for(dve, stats2, t, alone=True)
                    dve.bn_aggr(mv[:, 2 + t.c % 2, :], stats[:, 2 + t.c % 2, :]).then_inc(mv2, 1)
                if s.k is None and s.c < 2 * GROUP:
                    dve.memset(k_s[:, s.c // GROUP, s.c % GROUP, :], 0.0).then_inc(k_zeroed, 1)
                if s.k is None and s.c == LAG["score"] - 2:
                    ternary_weights()

            run(dve, step)

        @block.tensor
        def _(pe):
            pe.wait_ge(const_ready, 4)
            pe.wait_ge(w_loaded, 16 * 5)
            for i in range(5):
                if i == 3:
                    pe.wait_ge(wo_ordered, 1)
                w = wo_raw if i == 3 else w_raw[i]
                for kc in range(KC):
                    for oc in range(KC):
                        o = kc * D + oc * P
                        last = pe.transpose(w_bank[i][:, o:o + P], w[:, oc, kc * P:kc * P + P], ident[:, :])
                last.then_inc(w_transposed, 1)
            def values(a):
                b = a.c % 2
                wait_for(pe, v_placed, a, SQS)
                wait_for(pe, attn_kept, a.back(1))
                wait_for(pe, probs_turned, a)
                cells = p_value[:, 0:SLOTS * (HD + 1)].rearrange("p (q s d) -> p s q d", q=2, s=S4)
                for s4 in range(S4):
                    for c in range(GROUP):
                        last = pe.matmul(cells[32 * c:32 * c + SQ, s4, :, :], probs_t[:, b, GROUP * s4 + c, :],
                                         v_d[:, b, GROUP * s4 + c, :, :].rearrange("p q d -> p (q d)"),
                                         start=True, stop=True)
                last.then_inc(value_done, 1)

            def scores(a):
                gp, u = a.c // UNITS % 2, a.c % UNITS
                if u == 0:
                    wait_stacked(pe, stacked, a)
                wait_for(pe, shift_done, a.back(1))
                pe.matmul(p_score[:, :], mask_l[:, :], mask_r[:, :], start=True, stop=False)
                for s4 in range(S4):
                    for sq in range(SQS):
                        r = SLOTS * u + S4 * sq + s4
                        q = q_s[:, gp, :].rearrange("p (a r) -> p a r", r=R)[:, :, r]
                        k = k_s[:, gp, :, :].rearrange("p c (h t r) -> p c t h r", h=HEADS, t=T2)[:, :, :, :, r]
                        last = pe.matmul(p_score[32 * sq:32 * sq + SQ, L * s4:L * (s4 + 1)], q, k, start=False,
                                         stop=(s4 == S4 - 1))
                last.then_inc(scored, 1)

            PARTS = ((0, 0), (0, 1), (1, 0))

            def project(n, chunks):
                pair = n.c // 2 % 2
                if 0 in chunks:
                    if n.k is None and n.c == 0:
                        pe.wait_ge(w_hi, 3)
                        pe.wait_ge(w_ready, 3)
                    wait_for(pe, xc_lo, At(n.c // 2 * 2 + 1, n.k))
                    wait_for(pe, nat_ready, n.back(1), 3)
                for oc in chunks:
                    if oc == KC:
                        w, src, to, o = wv_t, KC, p_v[:, 0:2 * L], n.c % 2 * P
                    else:
                        w, src = ((wq_t, 0), (wk_t, KC))[n.c % 2]
                        to, o = p_proj[:, oc * 2 * L:(oc + 1) * 2 * L], oc * P
                    for kc in range(KC):
                        for ws, ms in PARTS:
                            last = pe.matmul(to, w[:, ws, kc, o:o + P], xc_t[:, pair, ms, src + kc, :],
                                             start=(kc == 0 and (ws, ms) == PARTS[0]),
                                             stop=(kc == KC - 1 and (ws, ms) == PARTS[-1]))
                    if oc >= KC - 1:
                        last.then_inc(v_projected if oc == KC else projected, 1)

            def step(s):
                t = batch(s, "transpose")
                if t:
                    wait_for(pe, xn_ready, t)
                    wait_parity(pe, c_loaded, t)
                    wait_for(pe, xc_lo, t.back(1))
                    for i in range(2 * KC):
                        src = (xn, c_in)[i // KC][:, t.c % 2, i % KC * P:i % KC * P + P]
                        last = pe.transpose(p_tr[:, i * L:(i + 1) * L], src, ident[:, :])
                    last.then_inc(xc_transposed, 1)
                a = batch(s, "score")
                if a:
                    scores(a)
                t = batch(s, "ffn")
                if t:
                    wait_for(pe, x1_lo, t)
                    wait_for(pe, y_ready, t.back(1))
                    for kc in range(KC):
                        for part in range(2):
                            last = pe.matmul(p_ffn[:, 0:D], x1_t[:, t.c % 2, part, kc * L:(kc + 1) * L],
                                             wf_t[:, kc * D:(kc + 1) * D], start=(kc + part == 0),
                                             stop=(kc == KC - 1 and part == 1))
                    last.then_inc(ffn_done, 1)
                a = batch(s, "value")
                if a:
                    values(a)
                n = batch(s, "project")
                if n:
                    project(n, range(KC))
                t = batch(s, "x1t")
                if t:
                    wait_for(pe, x1n_ready, t)
                    wait_for(pe, x1_lo, t.back(1))
                    for kc in range(KC):
                        last = pe.transpose(p_x1t[:, kc * L:(kc + 1) * L], x1n[:, t.c % 2, kc * P:kc * P + P],
                                            ident[:, :])
                    last.then_inc(x1_transposed, 1)
                if n:
                    project(n, [KC])
                t = batch(s, "out")
                if t:
                    wait_for(pe, x1_ready, t.back(1))
                    pe.matmul(p_out[:, 0:D], ones_r[:, 0:L], bias[:, :], start=True, stop=False)
                    wait_for(pe, attn_ordered, t)
                    for kc in range(KC):
                        last = pe.matmul(p_out[:, 0:D], attn_p[:, t.c % 2, kc * L:(kc + 1) * L],
                                         wo_t[:, kc * D:(kc + 1) * D], start=False, stop=(kc == KC - 1))
                    last.then_inc(out_done, 1)
                if s.k is None and s.c == 1:
                    pe.wait_ge(abs_summed, 1)
                    pe.wait_ge(dve_const, 1)
                    pe.matmul(p_ffn[:, 0:1], ones_f[:, :], scal[:, 0:1], start=True, stop=True).then_inc(abs_total, 1)
                if s.k is None and s.c == LAG["score"] - 1:
                    pe.wait_ge(const_ready, POOL_CONSTS)
                    pe.wait_ge(dve_const, 6)
                    pe.wait_ge(w_hi, 4)
                    pe.wait_ge(w_ready, 4)

            run(pe, step)


_INS = ["x", "ctx_1024", "g_xattn", "g_ffn", "L0_xattn_wq_w", "L0_xattn_wq_b", "L0_xattn_wk_w", "L0_xattn_wk_b",
        "L0_xattn_wv_w", "L0_xattn_wv_b", "L0_xattn_fo_w", "L0_xattn_fo_b", "L0_ffn_weight"]


def kernel(**inputs):
    import concourse.bacc as _bacc
    import numpy as _np
    from concourse.bass_utils import run_bass_kernel_spmd as _run

    nc = _bacc.Bacc("TRN2", target_bir_lowering=False, num_devices=1)
    arrays, args = {}, []
    for name in _INS:
        a = _np.ascontiguousarray(inputs[name])
        arrays[f"in_{name}"] = a
        args.append(nc.dram_tensor(f"in_{name}", a.shape, mybir.dt.from_np(a.dtype), kind="ExternalInput").ap())
    args.append(nc.dram_tensor("out_x", inputs["x"].shape, F32, kind="ExternalOutput").ap())
    batches, tokens, dim = inputs["x"].shape
    for name, shape in (("q", (batches // 2, 4 * dim // P, P, tokens // 2)),
                        ("k", (batches // 2, dim // P, P, 2 * tokens)),
                        ("v", (batches // 2, dim // P, P, 2 * tokens)),
                        ("attn", (batches // GROUP, P, HEADS * tokens // 2))):
        args.append(nc.dram_tensor(f"scratch_{name}", shape, F32, kind="Internal").ap())
    gated_block(nc, *args)
    r = _run(nc, [arrays], core_ids=[0])
    return r.results[0]["out_x"]
```

```python
from contextlib import ExitStack

import concourse.bass as bass
from concourse import mybir

F32 = mybir.dt.float32
F32R = mybir.dt.float32r
BF16 = mybir.dt.bfloat16
ALU = mybir.AluOpType
ACT = mybir.ActivationFunctionType
AX_X = mybir.AxisListType.X

P = 128
HEADS = 16
GROUP = 4
UNITS = 4
MASKED = -1e30
POOL_CONSTS = 9
KEYS_FILL = (2, 6)
Q_ZEROED, V_ZEROED, D_ZEROED = (1, 4), (2, 5), 3
LN_EPS = 1e-5
TERNARY_EPS = 1e-5

LAG = dict(ln1=0, transpose=1, project=2, score=7, value=8, out=12, x1t=13, ffn=14)
BODY = 8


class At:

    def __init__(self, c, k=None, per=BODY):
        self.c, self.k, self.per = c, k, per

    def back(self, n):
        return At(self.c - n, self.k, self.per)

    def over(self, n):
        return At(self.c // n, self.k, self.per // n)

    def value(self):
        return self.c if self.k is None else self.k * self.per + self.c


def count(at, per=1, extra=0):
    n = per * (at.c + 1) + extra
    if at.k is None:
        return n
    assert n > 0
    return at.k * (per * at.per) + n


def gated_block(nc, x, ctx, g_xattn, g_ffn, wq, bq, wk, bk, wv, bv, wo, bo, wf, out, q_dram, k_dram, v_dram,
                attn_dram):
    B, L, D = x.shape
    HD = D // HEADS
    KC = D // P
    T2 = 2
    SLOTS = L // UNITS // T2
    SQ = T2 * HEADS
    R = L // T2
    SQS = 4
    S4 = SLOTS // SQS
    S8 = SLOTS // 2
    HW = HEADS * L
    assert L == P and D == KC * P and HD == 16 and SQ == 32 and GROUP == UNITS == SQS and B % BODY == 0
    STEPS = B + LAG["ffn"]
    LOOP_FROM = 2 * BODY
    LOOPS = (B - LOOP_FROM) // BODY

    with ExitStack() as es:
        def sb(name, shape, dt=F32):
            return es.enter_context(nc.sbuf_tensor(name, shape, dt))

        def ps(name):
            return es.enter_context(nc.psum_tensor(name, [P, 512], F32))

        def sem(name):
            return es.enter_context(nc.semaphore(name))

        x_in = sb("x_in", [P, 2, D])
        c_in = sb("c_in", [P, 2, D])
        x_res = sb("x_res", [P, 2, D])
        xn = sb("xn", [P, 2, D])
        x1 = sb("x1", [P, 4, D])
        x1n = sb("x1n", [P, 2, D])
        y = sb("y", [P, 2, D])
        xc_t = sb("xc_t", [P, 2, 2, 2 * KC, 2 * L], F32R)
        x1_t = sb("x1_t", [P, 2, 2, KC * L], F32R)
        W2 = KC * 2 * L
        nat = sb("nat", [P, 2, 3 * W2])
        q_s = sb("q_s", [P, 2, HW])
        k_s = sb("k_s", [P, 2, GROUP, HW])
        v_s = sb("v_s", [P, 2, 2, HEADS, 2 * L // SQS])
        shifted = sb("shifted", [P, SLOTS, SQ])
        probs = sb("probs", [P, SLOTS, SQ])
        probs_t = sb("probs_t", [P, 2, SLOTS, SQ])
        v_t = sb("v_t", [P, 2, S4 * 2, SQ])
        v_d = sb("v_d", [P, 2, 2, S4 * 2, SQS, HD + 1])
        row_max = sb("row_max", [P, SLOTS])
        recip = sb("recip", [P, SLOTS])
        attn = sb("attn", [P, SLOTS * HD])
        attn_t = sb("attn_t", [P, 2, HEADS, R])
        attn_in = sb("attn_in", [P, GROUP, 2, KC, R])
        attn_p = sb("attn_p", [P, 2, KC * L])
        mask_l = sb("mask_l", [32, P], BF16)
        mask_r = sb("mask_r", [32, SLOTS * SQ], BF16)
        stats = sb("stats", [P, 4, 6])
        mv = sb("mv", [P, 4, 2])
        ln_c = sb("ln_c", [P, 4, 3])
        neg_half = sb("neg_half", [P, 1])
        ident = sb("ident", [P, P])
        ones_f = sb("ones_f", [P, P])
        ones_r = sb("ones_r", [P, L], F32R)
        wq_t = sb("wq_t", [P, 2, KC, D], F32R)
        wk_t = sb("wk_t", [P, 2, KC, D], F32R)
        wv_t = sb("wv_t", [P, 2, KC, D], F32R)
        wo_t = sb("wo_t", [P, KC * D])
        wf_t = sb("wf_t", [P, KC * D], F32R)
        bias_raw = sb("bias_raw", [2, D])
        bias_hi = sb("bias_hi", [2, D], F32R)
        bias = sb("bias", [P, D], F32R)
        bias_col = sb("bias_col", [P, 3 * KC])
        row_mask = sb("row_mask", [2, 1])
        gates = sb("gates", [P, 2])
        gates_t = sb("gates_t", [P, 2])
        scal = sb("scal", [P, 8])

        p_tr = ps("p_tr")
        p_x1t = ps("p_x1t")
        p_proj = ps("p_proj")
        p_v = ps("p_v")
        p_score = ps("p_score")
        p_value = ps("p_value")
        p_out = ps("p_out")
        p_ffn = ps("p_ffn")

        w_loaded = sem("w_loaded")
        w_loaded2 = sem("w_loaded2")
        bias_loaded = sem("bias_loaded")
        gates_loaded = sem("gates_loaded")
        x_loaded = [sem("x_loaded0"), sem("x_loaded1")]
        c_loaded = [sem("c_loaded0"), sem("c_loaded1")]
        res_loaded = [sem("res_loaded0"), sem("res_loaded1")]
        y_stored = [sem("y_stored0"), sem("y_stored1")]
        q_written = [sem("q_written0"), sem("q_written1")]
        k_written = [sem("k_written0"), sem("k_written1")]
        v_written = [sem("v_written0"), sem("v_written1")]
        stacked = [sem("stacked0"), sem("stacked1")]
        v_stacked = [sem("v_stacked0"), sem("v_stacked1")]
        attn_written = sem("attn_written")
        attn_loaded = [sem(f"attn_loaded{i}") for i in range(GROUP)]
        zeroed = sem("zeroed")
        k_zeroed = sem("k_zeroed")
        const_ready = sem("const_ready")
        dve_const = sem("dve_const")
        wo_ordered = sem("wo_ordered")
        w_transposed = sem("w_transposed")
        w_hi = sem("w_hi")
        abs_summed = sem("abs_summed")
        abs_total = sem("abs_total")
        setup_chain = sem("setup_chain")
        w_ready = sem("w_ready")
        gates_tanh = sem("gates_tanh")
        stats1 = sem("stats1")
        mv1 = sem("mv1")
        stats2 = sem("stats2")
        mv2 = sem("mv2")
        ln1_chain = sem("ln1_chain")
        ln2_chain = sem("ln2_chain")
        xn_ready = sem("xn_ready")
        x1n_ready = sem("x1n_ready")
        xc_transposed = sem("xc_transposed")
        xc_hi = sem("xc_hi")
        xc_lo = sem("xc_lo")
        projected = sem("projected")
        v_projected = sem("v_projected")
        nat_ready = sem("nat_ready")
        scored = sem("scored")
        max_done = sem("max_done")
        shift_done = sem("shift_done")
        exp_done = sem("exp_done")
        probs_turned = sem("probs_turned")
        v_turned = sem("v_turned")
        v_placed = sem("v_placed")
        value_done = sem("value_done")
        recip_done = sem("recip_done")
        attn_kept = sem("attn_kept")
        attn_turned = sem("attn_turned")
        attn_ordered = sem("attn_ordered")
        out_done = sem("out_done")
        x1_ready = sem("x1_ready")
        x1_transposed = sem("x1_transposed")
        x1_hi = sem("x1_hi")
        x1_lo = sem("x1_lo")
        ffn_done = sem("ffn_done")
        y_ready = sem("y_ready")

        weights = [wq, wk, wv, wo, wf]
        w_raw = [nat[:, i // 3, i % 3 * W2:(i % 3 + 1) * W2].rearrange("p (c d) -> p c d", c=KC) for i in range(5)]
        wo_raw = attn_t[:, 0, 0:KC * D // R, :].rearrange("p i r -> p (i r)").rearrange("p (c d) -> p c d", c=KC)
        w_bank = [p_proj, p_v, p_score, p_value, p_out]
        q_scale = float(HD) ** -0.5

        def wait_value(eng, s, value, alone):
            if alone:
                eng.compute_val(value)
                eng.wait_ge(const_ready, 1)
            eng.wait_ge(s, value)

        def wait_for(eng, s, at, per=1, extra=0, alone=False):
            if at.k is None:
                if at.c > B - 1:
                    at = At(B - 1)
                if count(at, per, extra) <= 0:
                    return
            wait_value(eng, s, count(at, per, extra), at.k is not None and (alone or eng is nc.gpsimd or eng is nc.sync))

        def wait_parity(eng, sems, at):
            if at.k is None and at.c < 0:
                return
            wait_value(eng, sems[at.c % 2], count(at.over(2), 16), at.k is not None and eng is nc.gpsimd)

        def wait_stacked(eng, sems, a):
            per = 16 * (GROUP if sems is v_stacked else 2 * GROUP)
            eng.wait_ge(sems[a.c // GROUP % 2], count(a.over(2 * GROUP), per))

        def batch(s, stage):
            t = s.back(LAG[stage])
            return t if t.k is not None or 0 <= t.c < B else None

        def is_late(s):
            return s.k is None and s.c >= B + LAG["value"]

        def run(eng, step):
            for s in range(LOOP_FROM):
                step(At(s))
            with eng.Fori(0, LOOPS) as k:
                for j in range(BODY):
                    step(At(LOOP_FROM + j, k))
            for s in range(LOOP_FROM + LOOPS * BODY, STEPS + 1):
                step(At(s))

        def rows(dram, t):
            return dram[bass.ds(t.value(), 1), :, :].rearrange("b l d -> l b d")

        block = es.enter_context(nc.Block())

        @block.sync
        def _(sp):
            def load_x(t):
                wait_for(sp, xn_ready, t.back(2))
                sp.dma_start(x_in[:, t.c % 2:t.c % 2 + 1, :], rows(x, t)).then_inc(x_loaded[t.c % 2], 16)

            def load_c(t):
                wait_for(sp, xc_transposed, t.back(2))
                sp.dma_start(c_in[:, t.c % 2:t.c % 2 + 1, :], rows(ctx, t)).then_inc(c_loaded[t.c % 2], 16)

            def load_weights(these, loaded):
                for i in these:
                    sp.dma_start(w_raw[i], weights[i].rearrange("(c p) d -> p c d", p=P)).then_inc(loaded, 16)

            load_x(At(0))
            load_c(At(0))
            load_weights(range(3), w_loaded)
            load_x(At(1))
            load_c(At(1))
            load_weights((3, 4), w_loaded2)
            for r in range(2):
                sp.dma_start(bias_raw[r:r + 1, :], bo.rearrange("(a d) -> a d", a=1)).then_inc(bias_loaded, 16)
            for i, b in enumerate((bq, bk, bv)):
                for c in range(KC):
                    sp.dma_start(bias_col[:, KC * i + c:KC * i + c + 1],
                                 b[c * P:c * P + P].rearrange("(p a) -> p a", a=1)).then_inc(bias_loaded, 16)
            def load_gates():
                for i, g in enumerate((g_xattn, g_ffn)):
                    sp.dma_start(gates[:, i:i + 1],
                                 g.rearrange("(a d) -> a d", a=1).to_broadcast([P, 1])).then_inc(gates_loaded, 16)

            def load_res(t):
                wait_for(sp, x1_ready, t.back(2))
                sp.dma_start(x_res[:, t.c % 2:t.c % 2 + 1, :], rows(x, t)).then_inc(res_loaded[t.c % 2], 16)

            def write_nat(n):
                b, p = n.c // 2 % 2, bass.ds(n.over(2).value(), 1)
                wait_for(sp, nat_ready, n, 3)
                if n.c % 2 == 0:
                    sp.dma_start(q_dram[p, :, :, :].rearrange("a m p r -> (a p) m r"),
                                 nat[:, b, 0:W2].rearrange("p (m r) -> p m r", r=R)).then_inc(q_written[b], 16)
                    return
                for dram, o, written in ((k_dram, W2, k_written), (v_dram, 2 * W2, v_written)):
                    sp.dma_start(dram[p, :, :, :].rearrange("a c p t -> (a p) c t"),
                                 nat[:, b, o:o + W2].rearrange("p (c t) -> p c t", c=KC)).then_inc(written[b], 16)

            def read_stacks(n):
                pair, g = n.over(2), n.over(GROUP)
                b, gp, at = n.c // 2 % 2, g.c % 2, bass.ds(pair.value(), 1)
                last = At(n.c // GROUP * GROUP - GROUP - 1, n.k)
                wait_for(sp, scored, last)
                fresh = n.k is None and n.c < 2 * GROUP
                if fresh:
                    sp.wait_ge(zeroed, Q_ZEROED[gp])
                    sp.wait_ge(k_zeroed, n.c + 1)
                batches = range(n.c // 2 * 2 % GROUP, n.c // 2 * 2 % GROUP + 2)
                wait_value(sp, q_written[b], count(g, 16), n.k is not None)
                for i, c in enumerate(batches):
                    sp.dma_start(q_s[32 * c:32 * c + HD, gp, :].rearrange("p (m r) -> p m r", r=R),
                                 q_dram[at, i * T2 * KC:(i + 1) * T2 * KC, :, :].rearrange(
                                     "a m (h p) r -> (a p) (m h) r", p=HD)).then_inc(stacked[gp], 16)
                wait_value(sp, k_written[b], count(g, 16), n.k is not None)
                for i, c in enumerate(batches):
                    sp.dma_start(k_s[32 * c:32 * c + HD, gp, c, :].rearrange("p (h t) -> p h t", h=HEADS),
                                 k_dram[at, :, :, i * L:i * L + L].rearrange("a s (h p) t -> (a p) (s h) t", p=HD)
                                 ).then_inc(stacked[gp], 16)
                if n.c % GROUP == GROUP - 1:
                    if fresh:
                        sp.wait_ge(zeroed, V_ZEROED[gp])
                    wait_for(sp, v_turned, last, 2)
                    wait_value(sp, v_written[0], count(g, 16), n.k is not None)
                    wait_value(sp, v_written[1], count(g, 16), n.k is not None)
                    pairs = v_dram[bass.ds(n.back(GROUP - 1).over(2).value(), 2), :, :, :]
                    W = 2 * L // SQS
                    for sq in range(SQS):
                        sp.dma_start(v_s[32 * sq:32 * sq + HD, gp, :, :, :].rearrange("p a h t -> p (a h) t"),
                                     pairs[:, :, :, sq * W:sq * W + W].rearrange("a s (h p) t -> p (a s h) t", p=HD)
                                     ).then_inc(v_stacked[gp], 16)

            def attn_back(a):
                g = a.over(GROUP)
                wait_for(sp, attn_turned, a)
                sp.dma_start(attn_dram[bass.ds(g.value(), 1), :, :].rearrange("a p m -> (a p) m"),
                             attn_t[:, g.c % 2, :, :].rearrange("p i r -> p (i r)")).then_inc(attn_written, 16)
                wait_value(sp, attn_written, count(g, 16), g.k is not None)
                there = attn_dram[bass.ds(g.value(), 1), :, :].rearrange("a p m -> (a p m)").rearrange(
                    "(b m p r) -> b p m r", b=GROUP, m=2 * KC, r=R)
                for c in range(GROUP):
                    wait_for(sp, attn_ordered, a.back(2 * GROUP - 1 - c))
                    sp.dma_start(attn_in[:, c, :, :, :].rearrange("p q c r -> p (q c) r"), there[c, :, :, :]
                                 ).then_inc(attn_loaded[c], 16)

            def step(s):
                n = s.back(LAG["project"] + 2)
                n = n if n.k is not None or 0 <= n.c < B else None
                early = s.k is None and s.c < LAG["score"]
                if n and not early:
                    write_nat(n)
                if s.k is not None or 2 <= s.c < B:
                    load_x(s)
                    load_c(s)
                if s.k is None and s.c == 3:
                    load_gates()
                if n and early:
                    write_nat(n)
                t = batch(s, "out")
                if t:
                    load_res(t)
                if n and n.c % 2 == 1:
                    read_stacks(n)
                t = s.back(LAG["ffn"] + 1)
                if t.k is not None or 0 <= t.c < B:
                    wait_for(sp, y_ready, t)
                    sp.dma_start(rows(out, t), y[:, t.c % 2:t.c % 2 + 1, :]).then_inc(y_stored[t.c % 2], 16)
                a = s.back(LAG["value"] + 1)
                if (a.k is not None or 0 <= a.c < B) and a.c % GROUP == GROUP - 1:
                    attn_back(a)

            run(sp, step)
            for i in range(2):
                sp.wait_ge(y_stored[i], 16 * (B // 2))

        @block.gpsimd
        def _(pool):
            pool.memset(ident[:, :], 0.0).then_inc(const_ready, 1)
            pool.memset(neg_half[:, :], -0.5).then_inc(const_ready, 1)
            pool.memset(row_mask[:, :], 0.0).then_inc(const_ready, 1)
            pool.wait_ge(const_ready, 3)
            pool.affine_select(out=ident[:, :], in_=ident[:, :], compare_op=ALU.not_equal, fill=1.0, base=0,
                               pattern=[[-1, P]], channel_multiplier=1).then_inc(const_ready, 1)
            pool.affine_select(out=row_mask[:, :], in_=row_mask[:, :], compare_op=ALU.not_equal, fill=-1.0, base=-1,
                               pattern=[[0, 1]], channel_multiplier=1).then_inc(const_ready, 1)
            pool.wait_ge(const_ready, 5)

            def masks():
                pool.memset(mask_l[:, :], 0.0).then_inc(const_ready, 1)
                pool.memset(mask_r[:, :], MASKED).then_inc(const_ready, 1)
                pool.wait_ge(const_ready, 7)
                pool.affine_select(out=mask_l[:, :], in_=mask_l[:, :], compare_op=ALU.not_equal, fill=1.0, base=0,
                                   pattern=[[0, GROUP], [-1, T2], [0, HEADS]], channel_multiplier=1).then_inc(const_ready, 1)
                pool.affine_select(out=mask_r[:, :], in_=mask_r[:, :], compare_op=ALU.not_equal, fill=0.0, base=0,
                                   pattern=[[0, SLOTS], [-1, T2], [0, HEADS]], channel_multiplier=1).then_inc(const_ready, 1)
                pool.wait_ge(const_ready, 9)

            def layer_norm(chain, src, dst, slot, t, base, per):
                c = ln_c[:, slot, :]
                nc.gpsimd.tensor_scalar(c[:, 0:1], mv[:, slot, 1:2], LN_EPS, None, ALU.add).then_inc(chain, 1)
                wait_for(pool, chain, t, per, base + 1 - per)
                nc.gpsimd.tensor_tensor(c[:, 1:2], c[:, 0:1], neg_half[:, :], ALU.pow).then_inc(chain, 1)
                wait_for(pool, chain, t, per, base + 2 - per)
                nc.gpsimd.tensor_scalar(c[:, 2:3], mv[:, slot, 0:1], c[:, 1:2], -1.0, ALU.mult, ALU.mult
                                        ).then_inc(chain, 1)
                wait_for(pool, chain, t, per, base + 3 - per)
                return nc.gpsimd.tensor_scalar(dst, src, c[:, 1:2], c[:, 2:3], ALU.mult, ALU.add)

            def step(s):
                t = batch(s, "ln1")
                if t:
                    wait_for(pool, mv1, t)
                    wait_parity(pool, x_loaded, t)
                    wait_for(pool, xc_transposed, t.back(2))
                    layer_norm(ln1_chain, x_in[:, t.c % 2, :], xn[:, t.c % 2, :], t.c % 2, t, 0, 3
                               ).then_inc(xn_ready, 1)
                t = batch(s, "out")
                if t:
                    wait_for(pool, mv2, t)
                    wait_for(pool, x1_ready, t)
                    wait_for(pool, x1_transposed, t.back(2))
                    layer_norm(ln2_chain, x1[:, t.c % 4, :], x1n[:, t.c % 2, :], 2 + t.c % 2, t, 0, 3
                               ).then_inc(x1n_ready, 1)
                if s.k is None and s.c == 1:
                    masks()
                fills = ((q_s[:, 0, :], 0.0), (v_s[:, 0, :, :, :], 1.0), (v_d[:, :, :, :, :, :], 0.0),
                         (q_s[:, 1, :], 0.0), (v_s[:, 1, :, :, :], 1.0))
                if s.k is None and 2 <= s.c < 2 + len(fills):
                    pool.memset(*fills[s.c - 2]).then_inc(zeroed, 1)

            run(pool, step)

        @block.scalar
        def _(act):
            def weights_qkv():
                for i, (w, scale) in enumerate(((wq_t, q_scale), (wk_t, 1.0), (wv_t, 1.0))):
                    act.wait_ge(w_transposed, i + 1)
                    act.activation(w[:, 0, :, :].rearrange("p c d -> p (c d)"), w_bank[i][:, :], ACT.Copy,
                                   scale=scale).then_inc(w_hi, 1)

            def weights_of():
                act.wait_ge(w_transposed, 4)
                act.activation(wo_t[:, :], w_bank[3][:, :], ACT.Copy).then_inc(w_hi, 1)
                act.wait_ge(gates_loaded, 32)
                act.activation(gates_t[:, :], gates[:, :], ACT.Tanh).then_inc(gates_tanh, 1)
                act.wait_ge(w_loaded2, 16 * 2)
                act.activation(shifted[:, :, :].rearrange("p s q -> p (s q)"),
                               w_raw[4].rearrange("p c d -> p (c d)"), ACT.Abs,
                               accum_out=scal[:, 0:1]).then_inc(abs_summed, 1)

            def order_attention(t):
                act.wait_ge(attn_loaded[t.c % GROUP], count(t.over(GROUP), 16))
                wait_for(act, out_done, t.back(2))
                act.activation(attn_p[:, t.c % 2, :].rearrange("p (m q s) -> p q m s", q=2, s=S4),
                               attn_in[:, t.c % GROUP, :, :, :].rearrange("p q c (m s) -> p q (c m) s", s=S4), ACT.Copy
                               ).then_inc(attn_ordered, 1)

            def step(s):
                late = is_late(s)
                t = batch(s, "transpose")
                if t:
                    wait_for(act, xc_transposed, t)
                    old = At(t.c // 2 * 2 - 3, t.k)
                    wait_for(act, projected, old)
                    wait_for(act, v_projected, old)
                    o = t.c % 2 * L
                    act.activation(xc_t[:, t.c // 2 % 2, 0, :, o:o + L],
                                   p_tr[:, :].rearrange("p (b l) -> p b l", b=2 * KC), ACT.Copy).then_inc(xc_hi, 1)
                a = batch(s, "value")
                if a:
                    wait_for(act, v_turned, a, 2)
                    wait_for(act, value_done, a.back(2))
                    if s.k is None and a.c < 2:
                        act.wait_ge(zeroed, D_ZEROED)
                    for sq in range(SQS):
                        h = slice(32 * sq, 32 * sq + 32)
                        act.activation(v_d[h, a.c % 2, :, :, sq, :].rearrange("p a s d -> p (a s) d"),
                                       v_t[h, :, :, 0:HD + 1].rearrange("p a s d -> p (a s) d"), ACT.Copy
                                       ).then_inc(v_placed, 1)
                a = batch(s, "score")
                if a:
                    wait_for(act, shift_done, a)
                    wait_for(act, probs_turned, a.back(1))
                    act.activation(probs[:, :, :], shifted[:, :, :], ACT.Exp).then_inc(exp_done, 1)
                t = batch(s, "out")
                if t and (late or t.c % GROUP > 0):
                    order_attention(t)
                t = batch(s, "x1t")
                if t:
                    wait_for(act, x1_transposed, t)
                    wait_for(act, ffn_done, t.back(2))
                    act.activation(x1_t[:, t.c % 2, 0, :], p_x1t[:, 0:KC * L], ACT.Copy).then_inc(x1_hi, 1)
                t = batch(s, "out")
                if t and not late and t.c % GROUP == 0:
                    order_attention(t)
                n = batch(s, "project")
                if n:
                    b, which = n.c // 2 % 2, n.c % 2
                    wait_for(act, projected, n)
                    if n.k is not None or n.c >= GROUP:
                        for written in ((q_written,), (k_written, v_written))[which]:
                            act.wait_ge(written[b], count(n.over(GROUP).back(1), 16))
                    if n.k is None and n.c == 0:
                        act.wait_ge(w_transposed, 3)
                        act.wait_ge(dve_const, 4)
                        act.wait_ge(bias_loaded, 16 * (2 + 3 * KC))
                    if n.k is None and n.c == 2:
                        act.wait_ge(w_transposed, 5)
                    for c in range(KC):
                        i = KC * which + c
                        to = nat[:, b, which * W2:(which + 1) * W2]
                        if which == 0:
                            to = to.rearrange("p (m c r) -> p c m r", c=KC, r=R)[:, c, :, :]
                        else:
                            to = to.rearrange("p (c m r) -> p c m r", c=KC, r=R)[:, c, :, :]
                        act.activation(to, p_proj[:, 2 * L * c:2 * L * (c + 1)].rearrange("p (m r) -> p m r", r=R),
                                       ACT.Identity, bias=bias_col[:, i:i + 1]).then_inc(nat_ready, 1)
                    i = 2 * KC + which
                    wait_for(act, v_projected, n)
                    act.activation(nat[:, b, i * 2 * L:(i + 1) * 2 * L].rearrange("p (q m s) -> p m q s", q=SQS, s=S4),
                                   p_v[:, 0:2 * L].rearrange("p (m q s) -> p m q s", q=SQS, s=S4), ACT.Identity,
                                   bias=bias_col[:, i:i + 1]).then_inc(nat_ready, 1)
                if s.k is None and s.c == 1:
                    weights_qkv()
                if s.k is None and s.c == 3:
                    weights_of()

            run(act, step)

        @block.vector
        def _(dve):
            dve.memset(ones_f[:, :], 1.0).then_inc(dve_const, 1)
            dve.memset(bias[:, :].bitcast(F32), 0.0).then_inc(dve_const, 1)
            dve.wait_ge(dve_const, 2)
            dve.tensor_copy(ones_r[:, 0:L], ones_f[:, :]).then_inc(dve_const, 1)

            def weights_setup():
                for i, (w, scale) in enumerate(((wq_t, q_scale), (wk_t, 1.0), (wv_t, 1.0))):
                    dve.wait_ge(w_hi, i + 1)
                    dve.scalar_tensor_tensor(out=w[:, 1, :, :].rearrange("p c d -> p (c d)"), in0=w_bank[i][:, :],
                                             scalar=scale, in1=w[:, 0, :, :].rearrange("p c d -> p (c d)").bitcast(F32),
                                             op0=ALU.mult, op1=ALU.subtract).then_inc(w_ready, 1)
                dve.wait_ge(bias_loaded, 16 * (2 + 3 * KC))
                dve.wait_ge(const_ready, 5)
                dve.tensor_scalar(bias_col[:, 0:KC], bias_col[:, 0:KC], q_scale, None, ALU.mult).then_inc(dve_const, 1)
                dve.tensor_copy(bias_hi[:, :], bias_raw[:, :]).then_inc(dve_const, 1)
                dve.wait_ge(dve_const, 5)
                dve.scalar_tensor_tensor(out=bias[0:2, :], in0=bias_hi[:, :].bitcast(F32), scalar=row_mask[:, 0:1],
                                         in1=bias_raw[:, :], op0=ALU.mult, op1=ALU.add).then_inc(dve_const, 1)
                dve.wait_ge(w_loaded2, 16 * 2)
                dve.tensor_copy(wo_raw.rearrange("p c (d i) -> p c d i", i=HEADS),
                                w_raw[3].rearrange("p c (i d) -> p c d i", i=HEADS)).then_inc(wo_ordered, 1)

            def ternary_weights():
                dve.wait_ge(abs_total, 1)
                dve.tensor_scalar(scal[:, 1:2], p_ffn[:, 0:1], 1.0 / (D * D), TERNARY_EPS, ALU.mult, ALU.max
                                  ).then_inc(setup_chain, 1)
                dve.wait_ge(setup_chain, 1)
                dve.tensor_scalar(scal[:, 2:3], scal[:, 1:2], 0.5, None, ALU.mult).then_inc(setup_chain, 1)
                dve.tensor_scalar(scal[:, 3:4], scal[:, 1:2], -0.5, None, ALU.mult).then_inc(setup_chain, 1)
                dve.wait_ge(gates_tanh, 1)
                dve.tensor_tensor(scal[:, 4:5], scal[:, 1:2], gates_t[:, 1:2], ALU.mult).then_inc(setup_chain, 1)
                dve.wait_ge(setup_chain, 4)
                dve.wait_ge(w_transposed, 5)
                above, below = (x1[:, i:i + 2, :].rearrange("p s q -> p (s q)") for i in (0, 2))
                dve.tensor_scalar(above, w_bank[4][:, :], scal[:, 2:3], None, ALU.is_gt).then_inc(setup_chain, 1)
                dve.tensor_scalar(below, w_bank[4][:, :], scal[:, 3:4], None, ALU.is_lt).then_inc(setup_chain, 1)
                dve.wait_ge(setup_chain, 6)
                dve.tensor_tensor(wf_t[:, :], above, below, ALU.subtract).then_inc(w_ready, 1)

            def stats_of_x(t):
                wait_parity(dve, x_loaded, t)
                wait_for(dve, xn_ready, t.back(2))
                dve.bn_stats(stats[:, t.c % 2, :], x_in[:, t.c % 2, :]).then_inc(stats1, 1)

            def aggregate(t):
                wait_for(dve, stats1, t, alone=True)
                dve.bn_aggr(mv[:, t.c % 2, :], stats[:, t.c % 2, :]).then_inc(mv1, 1)

            def turn_values(a):
                if a.c % UNITS == 0:
                    wait_stacked(dve, v_stacked, a)
                wait_for(dve, v_placed, a.back(1), SQS)
                o = S4 * (a.c % UNITS)
                for pair in range(2):
                    v = v_s[:, a.c // UNITS % 2, pair, :, :]
                    dve.transpose(v_t[:, pair, :, :].rearrange("p s q -> p (s q)"),
                                  v.rearrange("p h (t r) -> p r t h", t=2 * T2)[:, o:o + S4, :, :]
                                  ).then_inc(v_turned, 1)

            def output(t):
                wait_for(dve, ffn_done, t)
                wait_parity(dve, y_stored, t.back(2))
                wait_for(dve, x1_ready, t)
                dve.scalar_tensor_tensor(out=y[:, t.c % 2, :], in0=p_ffn[:, 0:D], scalar=scal[:, 4:5],
                                         in1=x1[:, t.c % 4, :], op0=ALU.mult, op1=ALU.add).then_inc(y_ready, 1)

            def low_of_x1(t):
                wait_for(dve, x1_hi, t)
                dve.tensor_tensor(x1_t[:, t.c % 2, 1, :], p_x1t[:, 0:KC * L],
                                  x1_t[:, t.c % 2, 0, :].bitcast(F32), ALU.subtract).then_inc(x1_lo, 1)

            def step(s):
                tx, a, late = batch(s, "ln1"), batch(s, "score"), is_late(s)
                early = s.k is None and s.c < LAG["score"]
                draining = s.k is None and s.c >= B
                if tx and early:
                    stats_of_x(tx)
                    aggregate(tx)
                t = batch(s, "transpose")
                if t:
                    o = t.c % 2 * L
                    wait_for(dve, xc_hi, t)
                    dve.tensor_tensor(xc_t[:, t.c // 2 % 2, 1, :, o:o + L],
                                      p_tr[:, :].rearrange("p (b l) -> p b l", b=2 * KC),
                                      xc_t[:, t.c // 2 % 2, 0, :, o:o + L].bitcast(F32), ALU.subtract
                                      ).then_inc(xc_lo, 1)
                if tx and not early:
                    stats_of_x(tx)
                if a:
                    wait_for(dve, scored, a)
                    dve.tensor_reduce(row_max[:, :], p_score[:, :].rearrange("p (s q) -> p s q", s=SLOTS), AX_X,
                                      ALU.max).then_inc(max_done, 1)
                if tx and not early:
                    aggregate(tx)
                if a:
                    wait_for(dve, max_done, a)
                    wait_for(dve, exp_done, a.back(1))
                    dve.tensor_tensor(shifted[:, :, :], p_score[:, :].rearrange("p (s q) -> p s q", s=SLOTS),
                                      row_max[:, :].rearrange("p (s a) -> p s a", a=1).to_broadcast([P, SLOTS, SQ]),
                                      ALU.subtract).then_inc(shift_done, 1)
                av = batch(s, "value")
                if av:
                    out3 = p_value[:, 0:SLOTS * (HD + 1)].rearrange("p (s d) -> p s d", s=SLOTS)
                    wait_for(dve, value_done, av)
                    dve.reciprocal(recip[:, :].rearrange("p (s a) -> p s a", a=1), out3[:, :, HD:HD + 1]
                                   ).then_inc(recip_done, 1)
                t = batch(s, "ffn")
                if t and not late:
                    output(t)
                if av:
                    wait_for(dve, recip_done, av)
                    dve.tensor_tensor(attn[:, :].rearrange("p (s d) -> p s d", s=SLOTS), out3[:, :, 0:HD],
                                      recip[:, :].rearrange("p (s a) -> p s a", a=1).to_broadcast([P, SLOTS, HD]),
                                      ALU.mult).then_inc(attn_kept, 1)
                if a:
                    wait_for(dve, exp_done, a)
                    wait_for(dve, value_done, a.back(2))
                    dve.transpose(probs_t[:, a.c % 2, :, :].rearrange("p s q -> p (s q)"),
                                  probs[:, :, :].rearrange("p s q -> p (s q)")).then_inc(probs_turned, 1)
                    if draining:
                        turn_values(a)
                if av:
                    wait_for(dve, attn_kept, av)
                    if av.c % UNITS == 0 and (av.k is not None or av.c >= 2 * GROUP):
                        dve.wait_ge(attn_written, count(av.over(GROUP).back(2), 16))
                    to = attn_t[:, av.c // UNITS % 2, :, :].rearrange("p i (t r) -> p r t i", t=T2)
                    u = av.c % UNITS
                    dve.transpose(to[:, S8 * u:S8 * u + S8, :, :], attn[:, :]).then_inc(attn_turned, 1)
                t = batch(s, "x1t")
                if t and not late:
                    low_of_x1(t)
                if a and not draining:
                    turn_values(a)
                t = batch(s, "out")
                if t:
                    wait_for(dve, out_done, t)
                    wait_parity(dve, res_loaded, t)
                    wait_for(dve, y_ready, t.back(4))
                    dve.scalar_tensor_tensor(out=x1[:, t.c % 4, :], in0=p_out[:, 0:D], scalar=gates_t[:, 0:1],
                                             in1=x_res[:, t.c % 2, :], op0=ALU.mult, op1=ALU.add
                                             ).then_inc(x1_ready, 1)
                    wait_for(dve, x1_ready, t)
                    wait_for(dve, x1n_ready, t.back(2))
                    dve.bn_stats(stats[:, 2 + t.c % 2, :], x1[:, t.c % 4, :]).then_inc(stats2, 1)
                    wait_for(dve, stats2, t, alone=True)
                    dve.bn_aggr(mv[:, 2 + t.c % 2, :], stats[:, 2 + t.c % 2, :]).then_inc(mv2, 1)
                t = batch(s, "x1t")
                if t and late:
                    low_of_x1(t)
                t = batch(s, "ffn")
                if t and late:
                    output(t)
                if s.k is None and s.c == 1:
                    weights_setup()
                for g, first in enumerate(KEYS_FILL):
                    if s.k is None and first <= s.c < first + GROUP:
                        dve.memset(k_s[:, g, s.c - first, :], 0.0).then_inc(k_zeroed, 1)
                if s.k is None and s.c == LAG["score"] + 4:
                    ternary_weights()

            run(dve, step)

        @block.tensor
        def _(pe):
            def turn_weights(these):
                pe.wait_ge(*((w_loaded, 16 * 3) if 0 in these else (w_loaded2, 16 * 2)))
                for i in these:
                    if i == 3:
                        pe.wait_ge(wo_ordered, 1)
                    w = wo_raw if i == 3 else w_raw[i]
                    for kc in range(KC):
                        for oc in range(KC):
                            o = kc * D + oc * P
                            last = pe.transpose(w_bank[i][:, o:o + P], w[:, oc, kc * P:kc * P + P], ident[:, :])
                    last.then_inc(w_transposed, 1)

            def values(a):
                b = a.c % 2
                wait_for(pe, v_placed, a, SQS)
                wait_for(pe, attn_kept, a.back(1))
                wait_for(pe, probs_turned, a)
                cells = p_value[:, 0:SLOTS * (HD + 1)].rearrange("p (q s d) -> p s q d", q=2, s=S4)
                for s4 in range(S4):
                    for c in range(GROUP):
                        last = pe.matmul(cells[32 * c:32 * c + SQ, s4, :, :], probs_t[:, b, GROUP * s4 + c, :],
                                         v_d[:, b, c // 2, 2 * s4 + c % 2, :, :].rearrange("p q d -> p (q d)"),
                                         start=True, stop=True)
                last.then_inc(value_done, 1)

            def scores(a):
                gp, u = a.c // UNITS % 2, a.c % UNITS
                if u == 0:
                    wait_stacked(pe, stacked, a)
                wait_for(pe, shift_done, a.back(1))
                pe.matmul(p_score[:, :], mask_l[:, :], mask_r[:, :], start=True, stop=False)
                for s4 in range(S4):
                    for sq in range(SQS):
                        r = SLOTS * u + S4 * sq + s4
                        q = q_s[:, gp, :].rearrange("p (a r) -> p a r", r=R)[:, :, r]
                        k = k_s[:, gp, :, :].rearrange("p c (h t r) -> p c t h r", h=HEADS, t=T2)[:, :, :, :, r]
                        last = pe.matmul(p_score[32 * sq:32 * sq + SQ, L * s4:L * (s4 + 1)], q, k, start=False,
                                         stop=(s4 == S4 - 1))
                last.then_inc(scored, 1)

            PARTS = ((0, 0), (0, 1), (1, 0))

            def project(n, chunks):
                pair = n.c // 2 % 2
                if 0 in chunks:
                    if n.k is None and n.c == 0:
                        pe.wait_ge(w_hi, 3)
                        pe.wait_ge(w_ready, 3)
                    wait_for(pe, xc_lo, At(n.c // 2 * 2 + 1, n.k))
                    wait_for(pe, nat_ready, n.back(1), 3)
                for oc in chunks:
                    if oc == KC:
                        w, src, to, o = wv_t, KC, p_v[:, 0:2 * L], n.c % 2 * P
                    else:
                        w, src = ((wq_t, 0), (wk_t, KC))[n.c % 2]
                        to, o = p_proj[:, oc * 2 * L:(oc + 1) * 2 * L], oc * P
                    for kc in range(KC):
                        for ws, ms in PARTS:
                            last = pe.matmul(to, w[:, ws, kc, o:o + P], xc_t[:, pair, ms, src + kc, :],
                                             start=(kc == 0 and (ws, ms) == PARTS[0]),
                                             stop=(kc == KC - 1 and (ws, ms) == PARTS[-1]))
                    if oc >= KC - 1:
                        last.then_inc(v_projected if oc == KC else projected, 1)

            def transpose_x1(t):
                wait_for(pe, x1n_ready, t)
                wait_for(pe, x1_lo, t.back(1))
                for kc in range(KC):
                    last = pe.transpose(p_x1t[:, kc * L:(kc + 1) * L], x1n[:, t.c % 2, kc * P:kc * P + P],
                                        ident[:, :])
                last.then_inc(x1_transposed, 1)

            def project_out(t):
                wait_for(pe, x1_ready, t.back(1))
                pe.matmul(p_out[:, 0:D], ones_r[:, 0:L], bias[:, :], start=True, stop=False)
                wait_for(pe, attn_ordered, t)
                for kc in range(KC):
                    last = pe.matmul(p_out[:, 0:D], attn_p[:, t.c % 2, kc * L:(kc + 1) * L],
                                     wo_t[:, kc * D:(kc + 1) * D], start=False, stop=(kc == KC - 1))
                last.then_inc(out_done, 1)

            def project_ffn(t):
                wait_for(pe, x1_lo, t)
                wait_for(pe, y_ready, t.back(1))
                for kc in range(KC):
                    for part in range(2):
                        last = pe.matmul(p_ffn[:, 0:D], x1_t[:, t.c % 2, part, kc * L:(kc + 1) * L],
                                         wf_t[:, kc * D:(kc + 1) * D], start=(kc + part == 0),
                                         stop=(kc == KC - 1 and part == 1))
                last.then_inc(ffn_done, 1)

            def step(s):
                late = is_late(s)
                t = batch(s, "transpose")
                if t:
                    if s.k is None and t.c == 0:
                        pe.wait_ge(const_ready, 4)
                    wait_for(pe, xn_ready, t)
                    wait_parity(pe, c_loaded, t)
                    wait_for(pe, xc_lo, t.back(1))
                    for i in range(2 * KC):
                        src = (xn, c_in)[i // KC][:, t.c % 2, i % KC * P:i % KC * P + P]
                        last = pe.transpose(p_tr[:, i * L:(i + 1) * L], src, ident[:, :])
                    last.then_inc(xc_transposed, 1)
                a = batch(s, "score")
                if a:
                    scores(a)
                t = batch(s, "ffn")
                if t and not late:
                    project_ffn(t)
                a = batch(s, "value")
                if a:
                    values(a)
                n = batch(s, "project")
                if n:
                    project(n, range(KC))
                t = batch(s, "x1t")
                if t and not late:
                    transpose_x1(t)
                if n:
                    project(n, [KC])
                t = batch(s, "out")
                if t:
                    project_out(t)
                t = batch(s, "x1t")
                if t and late:
                    transpose_x1(t)
                t = batch(s, "ffn")
                if t and late:
                    project_ffn(t)
                if s.k is None and s.c == 1:
                    turn_weights(range(3))
                if s.k is None and s.c == 3:
                    turn_weights((3, 4))
                if s.k is None and s.c == 4:
                    pe.wait_ge(abs_summed, 1)
                    pe.wait_ge(dve_const, 1)
                    pe.matmul(p_ffn[:, 0:1], ones_f[:, :], scal[:, 0:1], start=True, stop=True
                              ).then_inc(abs_total, 1)
                if s.k is None and s.c == LAG["score"] - 1:
                    pe.wait_ge(const_ready, POOL_CONSTS)
                if s.k is None and s.c == LAG["out"] - 1:
                    pe.wait_ge(dve_const, 6)
                    pe.wait_ge(w_hi, 4)
                if s.k is None and s.c == LAG["ffn"] - 1:
                    pe.wait_ge(w_ready, 4)

            run(pe, step)


_INS = ["x", "ctx_1024", "g_xattn", "g_ffn", "L0_xattn_wq_w", "L0_xattn_wq_b", "L0_xattn_wk_w", "L0_xattn_wk_b",
        "L0_xattn_wv_w", "L0_xattn_wv_b", "L0_xattn_fo_w", "L0_xattn_fo_b", "L0_ffn_weight"]


def kernel(**inputs):
    import concourse.bacc as _bacc
    import numpy as _np
    from concourse.bass_utils import run_bass_kernel_spmd as _run

    nc = _bacc.Bacc("TRN2", target_bir_lowering=False, num_devices=1)
    arrays, args = {}, []
    for name in _INS:
        a = _np.ascontiguousarray(inputs[name])
        arrays[f"in_{name}"] = a
        args.append(nc.dram_tensor(f"in_{name}", a.shape, mybir.dt.from_np(a.dtype), kind="ExternalInput").ap())
    args.append(nc.dram_tensor("out_x", inputs["x"].shape, F32, kind="ExternalOutput").ap())
    batches, tokens, dim = inputs["x"].shape
    for name, shape in (("q", (batches // 2, 4 * dim // P, P, tokens // 2)),
                        ("k", (batches // 2, dim // P, P, 2 * tokens)),
                        ("v", (batches // 2, dim // P, P, 2 * tokens)),
                        ("attn", (batches // GROUP, P, HEADS * tokens // 2))):
        args.append(nc.dram_tensor(f"scratch_{name}", shape, F32, kind="Internal").ap())
    gated_block(nc, *args)
    r = _run(nc, [arrays], core_ids=[0])
    return r.results[0]["out_x"]
```
